# Optimizing a Trainium2 kernel written in Bass

```python
import numpy as np
import jax
import jax.numpy as jnp

def _softmax(x, axis=-1):
    return jax.nn.softmax(x, axis=axis)

def _gelu(x):
    return jax.nn.gelu(x, approximate=True)

def _silu(x):
    return jax.nn.silu(x)

def _sigmoid(x):
    return jax.nn.sigmoid(x)

def _layernorm(x, axis=-1, eps=1e-05):
    m = jnp.mean(x, axis=axis, keepdims=True)
    v = jnp.var(x, axis=axis, keepdims=True)
    return (x - m) / jnp.sqrt(v + eps)

def _scatter_add(tgt, idx, src, axis=0):
    return tgt.at[idx].add(src)

def _segment_sum(src, seg, n):
    return jax.ops.segment_sum(src, seg, n)
kernel_name = 'mk_xattn_ffn_d1_seqx_r4_00b82a'

def setup_inputs(seed: int=0):
    np.random.seed(seed)
    _w = jnp.asarray

    def _rec_inputs():
        import jax
        import jax.numpy as jnp
        _rk = jax.random.key(seed)
        x = -0.0003929 + 0.9999 * jax.random.normal(jax.random.fold_in(_rk, 1), (8, 100, 512), jnp.float32)
        _lenS = 100 - jax.random.randint(jax.random.fold_in(_rk, 7), (8,), 0, max(1, 100 // 4) + 1, jnp.int32)
        _lenS2 = 361 - jax.random.randint(jax.random.fold_in(_rk, 8), (8,), 0, max(1, 361 // 4) + 1, jnp.int32)
        _ctx_2048P = jax.random.normal(jax.random.fold_in(_rk, 11), (8, 16, 512), jnp.float32)
        _ctx_2048c = jax.random.dirichlet(jax.random.fold_in(_rk, 511), 0.3 * jnp.ones((16,), jnp.float32), (8, 361))
        _ctx_2048t = jnp.einsum('bsk,bkd->bsd', _ctx_2048c, _ctx_2048P)
        _ctx_2048t = _ctx_2048t * jax.lax.rsqrt(jnp.mean(jnp.square(_ctx_2048t)) + 1e-12) * 0.953939
        ctx_2048 = -0.000514642 + 1.00011 * (_ctx_2048t + 0.3 * jax.random.normal(jax.random.fold_in(_rk, 611), (8, 361, 512), jnp.float32))
        return (x, ctx_2048)
    x, ctx_2048 = _rec_inputs()

    def _L0_xattn_setup():
        import jax, jax.numpy as jnp
        import numpy as np
        DIM = 512
        NHEADS = 32
        HEAD_DIM = DIM // NHEADS
        EPS = 1e-06

        def _rmsnorm(t):
            return t * jax.lax.rsqrt(jnp.mean(t * t, axis=-1, keepdims=True) + EPS)
        key = jax.random.key(seed)
        kx, kc, kq, kk, kv = jax.random.split(key, 5)
        x = jax.random.normal(kx, (2, 1024, DIM), dtype=jnp.float32)
        context = jax.random.normal(kc, (2, 128, DIM), dtype=jnp.float32)
        std = 0.02
        Wq = jax.random.normal(kq, (DIM, DIM), dtype=jnp.float32) * std
        Wk = jax.random.normal(kk, (DIM, DIM), dtype=jnp.float32) * std
        Wv = jax.random.normal(kv, (DIM, DIM), dtype=jnp.float32) * std
        return {'x': x, 'context': context, 'Wq': Wq, 'Wk': Wk, 'Wv': Wv}
    _L0_xattn_all = _L0_xattn_setup()
    _L0_xattn_in = {k: v for k, v in _L0_xattn_all.items() if k in ('Wq', 'Wk', 'Wv')}
    del _L0_xattn_all

    def _L0_ffn_setup():
        import jax, jax.numpy as jnp
        import numpy as np
        B, S, D = (2, 512, 512)
        MOE_D = 352
        E = 16
        K = 6
        ALPHA = 0.001

        def _moe_forward(x, gate_w, w_gate, w_up, w_down):
            b, s, d = x.shape
            T = b * s
            h = x.reshape(T, d)
            logits = h @ gate_w.T
            scores = jax.nn.softmax(logits.astype(jnp.float32), axis=-1)
            topk_w, topk_idx = jax.lax.top_k(scores, K)
            cw = jnp.zeros((T, E), jnp.float32)
            cw = cw.at[jnp.arange(T)[:, None], topk_idx].add(topk_w)
            y = jnp.zeros((T, d), x.dtype)
            for e in range(E):
                g = h @ w_gate[e].T
                u = h @ w_up[e].T
                out = jax.nn.silu(g) * u @ w_down[e].T
                y = y + cw[:, e:e + 1].astype(x.dtype) * out
            counts = jnp.sum(jax.nn.one_hot(topk_idx.reshape(b, s * K), E, dtype=jnp.float32), axis=1)
            ce = counts * (E / (s * K))
            scores_bse = scores.reshape(b, s, E)
            aux = jnp.mean(jnp.sum(ce * scores_bse.mean(axis=1), axis=1)) * ALPHA
            return (y.reshape(b, s, d), aux)
        key = jax.random.key(seed)
        ks = jax.random.split(key, 5)
        sd = 1.0 / np.sqrt(D)
        sm = 1.0 / np.sqrt(MOE_D)
        return {'x': jax.random.normal(ks[0], (B, S, D), jnp.float32), 'gate_w': jax.random.normal(ks[1], (E, D), jnp.float32) * sd, 'w_gate': jax.random.normal(ks[2], (E, MOE_D, D), jnp.float32) * sd, 'w_up': jax.random.normal(ks[3], (E, MOE_D, D), jnp.float32) * sd, 'w_down': jax.random.normal(ks[4], (E, D, MOE_D), jnp.float32) * sm}
    _L0_ffn_all = _L0_ffn_setup()
    _L0_ffn_in = {k: v for k, v in _L0_ffn_all.items() if k in ('gate_w', 'w_gate', 'w_up', 'w_down')}
    del _L0_ffn_all
    return {'x': x, 'ctx_2048': ctx_2048, 'L0_xattn_Wq': _L0_xattn_in['Wq'], 'L0_xattn_Wk': _L0_xattn_in['Wk'], 'L0_xattn_Wv': _L0_xattn_in['Wv'], 'L0_ffn_gate_w': _L0_ffn_in['gate_w'], 'L0_ffn_w_gate': _L0_ffn_in['w_gate'], 'L0_ffn_w_up': _L0_ffn_in['w_up'], 'L0_ffn_w_down': _L0_ffn_in['w_down']}

def reference(x, ctx_2048, L0_xattn_Wq, L0_xattn_Wk, L0_xattn_Wv, L0_ffn_gate_w, L0_ffn_w_gate, L0_ffn_w_up, L0_ffn_w_down):
    import jax
    import jax.numpy as jnp

    def _L0_xattn_ref(x, context, Wq, Wk, Wv):
        import jax, jax.numpy as jnp
        import numpy as np
        DIM = 512
        NHEADS = 32
        HEAD_DIM = DIM // NHEADS
        EPS = 1e-06

        def _rmsnorm(t):
            return t * jax.lax.rsqrt(jnp.mean(t * t, axis=-1, keepdims=True) + EPS)
        b, n, _ = x.shape
        m = context.shape[1]
        q = x @ Wq.T
        k_raw = context @ Wk.T
        v_raw = context @ Wv.T
        q = q.reshape(b, n, NHEADS, HEAD_DIM).transpose(0, 2, 1, 3)
        kv = jnp.concatenate([k_raw, v_raw], axis=-1)
        kv = kv.reshape(b, m, NHEADS, HEAD_DIM, 2)
        k = kv[..., 0].transpose(0, 2, 1, 3)
        v = kv[..., 1].transpose(0, 2, 1, 3)
        q = _rmsnorm(q)
        k = _rmsnorm(k)
        scale = HEAD_DIM ** (-0.5)
        scores = jnp.einsum('bhnd,bhmd->bhnm', q, k) * scale
        attn = jax.nn.softmax(scores, axis=-1)
        out = jnp.einsum('bhnm,bhmd->bhnd', attn, v)
        return out.transpose(0, 2, 1, 3).reshape(b, n, NHEADS * HEAD_DIM)

    def _L0_ffn_ref(x, gate_w, w_gate, w_up, w_down):
        import jax, jax.numpy as jnp
        import numpy as np
        B, S, D = (2, 512, 512)
        MOE_D = 352
        E = 16
        K = 6
        ALPHA = 0.001

        def _moe_forward(x, gate_w, w_gate, w_up, w_down):
            b, s, d = x.shape
            T = b * s
            h = x.reshape(T, d)
            logits = h @ gate_w.T
            scores = jax.nn.softmax(logits.astype(jnp.float32), axis=-1)
            topk_w, topk_idx = jax.lax.top_k(scores, K)
            cw = jnp.zeros((T, E), jnp.float32)
            cw = cw.at[jnp.arange(T)[:, None], topk_idx].add(topk_w)
            y = jnp.zeros((T, d), x.dtype)
            for e in range(E):
                g = h @ w_gate[e].T
                u = h @ w_up[e].T
                out = jax.nn.silu(g) * u @ w_down[e].T
                y = y + cw[:, e:e + 1].astype(x.dtype) * out
            counts = jnp.sum(jax.nn.one_hot(topk_idx.reshape(b, s * K), E, dtype=jnp.float32), axis=1)
            ce = counts * (E / (s * K))
            scores_bse = scores.reshape(b, s, E)
            aux = jnp.mean(jnp.sum(ce * scores_bse.mean(axis=1), axis=1)) * ALPHA
            return (y.reshape(b, s, d), aux)
        y, _aux = _moe_forward(x, gate_w, w_gate, w_up, w_down)
        return y
    x = x + _L0_xattn_ref(_layernorm(x, axis=-1), ctx_2048, L0_xattn_Wq, L0_xattn_Wk, L0_xattn_Wv)
    x = x + _L0_ffn_ref(_layernorm(x, axis=-1), L0_ffn_gate_w, L0_ffn_w_gate, L0_ffn_w_up, L0_ffn_w_down)
    return x

_drawn_inputs = setup_inputs


def setup_inputs(seed=0):
    import zlib

    import numpy as np

    out = dict(_drawn_inputs(seed))
    spreads = {}
    factors = {}
    for name, (base, spread) in spreads.items():
        noise = np.random.default_rng([zlib.crc32(name.encode()), seed]).standard_normal(out[name].shape)
        drawn = base * np.exp(spread * noise) if base else spread * noise
        out[name] = jnp.asarray(drawn.astype(out[name].dtype))
    for name, factor in factors.items():
        out[name] = (out[name] * factor).astype(out[name].dtype)
    return out
```

```python
from contextlib import ExitStack

import concourse.bass as bass
from concourse import mybir

F32 = mybir.dt.float32
F32R = mybir.dt.float32r
F16 = mybir.dt.float16
ALU = mybir.AluOpType
ACT = mybir.ActivationFunctionType
AX = mybir.AxisListType

P = 128
LN_EPS = 1e-5
RMS_EPS = 1e-6
TOP_K = 6


def xattn_moe_program(nc, x, ctx_t, w_kvq, gate_t, w_moe, eye, out_t):
    B, N, D = x.shape
    _, _, KT, M = ctx_t.shape
    E = gate_t.shape[2]
    TILES = w_moe.shape[0]
    FE = TILES * P // E
    H = 32
    HD = D // H
    HV = HD + 1
    T = B * N
    NH = T // 2
    MT = [(0, P), (P, P), (2 * P, M - 2 * P)]
    PAIRS = H // 2
    HG = 4
    GH = H // HG
    UNITS = HG * len(MT)
    KQ = 4
    TR = 9
    PER = 11
    EPER = PER * P // FE
    ITER = TILES // PER
    assert PER * P == EPER * FE and ITER * PER == TILES and D == KT * P and T == 2 * NH
    GROUPS = [(0, 4), (4, 8), (8, 11)]
    HSLOT = [0, 1, 2, 3, 4, 5, 6, 7, 1, 2, 3]
    WR = 4
    CASES = [(0, 0), (0, 1), (1, 0)]

    scratch = nc.dram_tensor("combine_scratch", (E, T), F32, kind="Internal").ap()

    with ExitStack() as ctx:
        def sem(name):
            return ctx.enter_context(nc.semaphore(name))

        def tensors(stack):
            return (lambda name, shape, dt=F32: stack.enter_context(nc.sbuf_tensor(name, shape, dt)),
                    lambda name, shape, dt=F32: stack.enter_context(nc.psum_tensor(name, shape, dt)))

        staging = ExitStack()
        sb, _ = tensors(staging)
        w_raw = sb("w_raw", [P, 3, KT, D])
        staging.close()

        sb, _ = tensors(ctx)
        y_sum = sb("y_sum", [P, KT, T])
        h_parts = [sb("h_hi", [P, KT, T], F32R), sb("h_lo", [P, KT, T], F32R)]
        id32 = sb("id32", [P, P])
        id16 = sb("id16", [P, P], F16)
        gate_w = sb("gate_w", [P, KT, E])
        cw = sb("cw", [N, E])
        cw_t = sb("cw_t", [E, T])
        minus_half = sb("minus_half", [P, H])
        rms_eps = sb("rms_eps", [P, H])
        ln_eps = sb("ln_eps", [P, 1])
        carrier = sb("carrier", [1, 1])

        att = ExitStack()
        sb, ps = tensors(att)
        w_parts = [sb("w_hi", [P, 3, KT, D], F32R), sb("w_lo", [P, 3, KT, D], F32R)]
        c_raw = sb("c_raw", [P, KT, M])
        c_parts = [sb("c_hi", [P, KT, M], F32R), sb("c_lo", [P, KT, M], F32R)]
        xin = sb("xin", [N, D])
        xres = sb("xres", [N, D])
        xn = sb("xn", [N, D])
        xt = sb("xt", [P, KT, N])
        x_parts = [sb("xt_hi", [P, KT, N], F32R), sb("xt_lo", [P, KT, N], F32R)]
        stats_x, mv_x, rstd_xb = sb("stats_x", [N, 6]), sb("mv_x", [N, 2]), sb("rstd_xb", [N, 2])
        stats_h, mv_h, rstd_hb = sb("stats_h", [N, 6]), sb("mv_h", [N, 2]), sb("rstd_hb", [N, 2])
        sq = sb("sq", [P, D])
        ss = sb("ss", [P, 2, H])
        ms = sb("ms", [P, H])
        rinv = sb("rinv", [P, 2, H])
        kn = sb("kn", [P, D])
        stack4 = [sb(f"stack4_{i}", [P, H, 4, HD], F16) for i in range(2)]
        k_t = [sb(f"k_t{i}", [P, PAIRS, M], F16) for i in range(2)]
        q_blk = [sb(f"q_blk{i}", [P, PAIRS, 2 * N], F16) for i in range(2)]
        v_ext = [sb(f"v_ext{i}", [P, 3, H, HV]) for i in range(2)]
        probs = [sb(f"probs{i}", [P, GH * N]) for i in range(2)]
        o_inv = sb("o_inv", [N, 2, GH])
        x1 = [sb(f"x1_{i}", [N, D]) for i in range(2)]
        hn = sb("hn", [N, D])
        ht = sb("ht", [P, KT, N])
        lg = sb("lg", [N, E])
        top_l = sb("top_l", [N, 8])
        neg_m = sb("neg_m", [N, 1])
        pexp = sb("pexp", [N, E])
        pinv = sb("pinv", [N, 2])
        sc_ext = sb("sc_ext", [N, E + 2])
        top_s = sb("top_s", [N, 8])
        rest = sb("rest", [N, E + 2])
        s_bank = ps("s_bank", [P, 2, 512])
        kq_bank = ps("kq_bank", [P, 2, 512])
        o_bank = ps("o_bank", [P, 2, 512])
        tr_bank = ps("tr_bank", [P, 1024], F16)
        v_bank = ps("v_bank", [P, 512])
        att.close()

        sb, ps = tensors(ctx)
        raw = [sb(f"raw{i}", [P, 3 * D]) for i in range(WR)]
        gu_parts = [[sb(f"gu_hi{i}", [P, 2, KT, P], F32R), sb(f"gu_lo{i}", [P, 2, KT, P], F32R)] for i in range(WR)]
        dn_parts = [[sb(f"dn_hi{i}", [P, D], F32R), sb(f"dn_lo{i}", [P, D], F32R)] for i in range(8)]
        a_parts = [[sb(f"a_hi{i}", [P, T], F32R), sb(f"a_lo{i}", [P, T], F32R)] for i in range(8)]
        cw_b = [sb(f"cw_b{i}", [P, T]) for i in range(EPER)]
        act_g = [sb(f"act_g{i}", [P, NH]) for i in range(2)]
        act_u = [sb(f"act_u{i}", [P, NH]) for i in range(2)]
        act_f = [sb(f"act_f{i}", [P, NH]) for i in range(2)]
        g_bank = ps("g_bank", [P, 2, 512])
        u_bank = ps("u_bank", [P, 2, 512])
        y_bank = ps("y_bank", [P, 4, 512])

        eye_in, gate_in = sem("eye_in"), sem("gate_in")
        w_in = [sem(f"w_in{i}") for i in range(3)]
        ctx_in, x_in, xres_in = sem("ctx_in"), sem("x_in"), sem("xres_in")
        consts = sem("consts")
        id16_made = sem("id16_made")
        w_hi_made, w_lo_made = sem("w_hi_made"), sem("w_lo_made")
        c_hi_made, c_lo_made = sem("c_hi_made"), sem("c_lo_made")
        bn_x, var_x, rstd_x, xn_made = sem("bn_x"), sem("var_x"), sem("rstd_x"), sem("xn_made")
        xt_made, x_hi_made, x_lo_made = sem("xt_made"), sem("x_hi_made"), sem("x_lo_made")
        kq_done, v_done = sem("kq_done"), sem("v_done")
        sq_made, ss_made, ms_made, rinv_made = sem("sq_made"), sem("ss_made"), sem("ms_made"), sem("rinv_made")
        kn_made, p_hi_made, p_lo_made = sem("kn_made"), sem("p_hi_made"), sem("p_lo_made")
        v_copied = sem("v_copied")
        tr_done, tr_used = sem("tr_done"), sem("tr_used")
        scores_done, probs_made, pv_done, o_normed = sem("scores_done"), sem("probs_made"), sem("pv_done"), sem("o_normed")
        o_inv_made, x1_made = sem("o_inv_made"), sem("x1_made")
        bn_h, var_h, rstd_h, hn_made = sem("bn_h"), sem("var_h"), sem("rstd_h"), sem("hn_made")
        ht_done, ht_made, h_hi_made, h_lo_made = sem("ht_done"), sem("ht_made"), sem("h_hi_made"), sem("h_lo_made")
        x1t_done, x1t_made = sem("x1t_done"), sem("x1t_made")
        lg_done, lg_made, negm_made, pexp_made = sem("lg_done"), sem("lg_made"), sem("negm_made"), sem("pexp_made")
        gate_step, cw_made, cwt_done, cwt_made = sem("gate_step"), sem("cw_made"), sem("cwt_done"), sem("cwt_made")
        rest_made = sem("rest_made")
        scratch_written = sem("scratch_written")
        raw_in = [sem(f"raw_in{i}") for i in range(WR)]
        cwb_in = [sem(f"cwb_in{i}") for i in range(EPER)]
        gu_hi_made, gu_lo_made, dn_hi_made, dn_lo_made = sem("gu_hi_made"), sem("gu_lo_made"), sem("dn_hi_made"), sem("dn_lo_made")
        g_done, u_done = sem("g_done"), sem("u_done")
        silu_made, gu_mult, af_made, a_hi_made, a_lo_made = sem("silu_made"), sem("gu_mult"), sem("af_made"), sem("a_hi_made"), sem("a_lo_made")
        y_done, y_added, out_written = sem("y_done"), sem("y_added"), sem("out_written")

        block = ctx.enter_context(nc.Block())

        def wait(eng, semaphore, value):
            if not isinstance(value, int) or value > 0:
                eng.wait_ge(semaphore, value)

        def carry_wait():
            nc.vector.memset(carrier[:, :], 0.0)

        def batches(eng, one):
            one(None, 1, 0, None)
            one(0, 0, 1, None)
            with eng.Fori(0, (B - 2) // 2) as i:
                one(i * 2 + 1, 1, i * 2 + 2, i * 2)
                one(i * 2 + 2, 0, i * 2 + 3, i * 2 + 1)
            one(B - 1, 1, None, B - 2)

        def hidden_tiles(eng, one, group):
            def round_(i, more):
                for p in range(1, PER):
                    one(i, p)
                    if p == 4:
                        group(i, 0)
                    if p == 8:
                        group(i, 1)
                if more:
                    one(i + 1, 0)
                group(i, 2)
            one(0, 0)
            with eng.Fori(0, ITER - 1) as i:
                round_(i, True)
            round_(ITER - 1, False)

        ITEM = [(0, MT[0][1]), (0, MT[1][1]), (2, N), (0, MT[2][1])]
        LAST_TR = [2, 5, 7, 9]

        def parts_free(n, item):
            return TR * n + LAST_TR[item - 2] - (TR if item < 2 else 0)

        def slot_user(p):
            return p - WR if p >= WR else max(q for q in range(PER) if q % WR == p % WR) - PER

        def loads(i, p):
            return i * len([q for q in range(PER) if q % WR == p % WR]) + p // WR + 1

        def cw_segments(p):
            cuts = {0, P} | {e * FE - p * P for e in range(EPER) if 0 < e * FE - p * P < P}
            if 32 in cuts:
                cuts.add(64)
            cuts = sorted(cuts)
            return [(a, b, (p * P + a) // FE) for a, b in zip(cuts, cuts[1:])]

        @block.sync
        def _(sp):
            sp.dma_start(c_raw[:, :, :], ctx_t[0]).then_inc(ctx_in, 16)
            for j in range(3):
                sp.dma_start(w_raw[:, j, :, :], w_kvq[:, j, :, :]).then_inc(w_in[j], 16)
            sp.dma_start(id32[:, :], eye).then_inc(eye_in, 16)
            sp.dma_start(xin[:, :], x[0]).then_inc(x_in, 16)
            sp.dma_start(gate_w[:, :, :], gate_t).then_inc(gate_in, 16)
            with sp.Fori(1, B) as n:
                sp.wait_ge(c_hi_made, n)
                sp.wait_ge(c_lo_made, n)
                sp.dma_start(c_raw[:, :, :], ctx_t[bass.ds(n, 1)].rearrange("o p k m -> (o p) k m")).then_inc(ctx_in, 16)
                sp.wait_ge(xn_made, n)
                sp.dma_start(xin[:, :], x[bass.ds(n, 1)].rearrange("o t d -> (o t) d")).then_inc(x_in, 16)
            sp.wait_ge(kq_done, KQ * B)
            sp.wait_ge(v_done, 3 * B)
            for t in range(WR):
                sp.dma_start(raw[t][:, :], w_moe[t]).then_inc(raw_in[t], 16)
            sp.wait_ge(cwt_made, B)
            sp.dma_start(scratch, cw_t[:, :]).then_inc(scratch_written, 16)
            sp.wait_ge(scratch_written, 16)
            for e in range(EPER):
                sp.dma_start(cw_b[e][:, :], scratch[e].partition_broadcast(P)).then_inc(cwb_in[e], 16)

            def load_round(i, last):
                for q in range(PER - WR if last else PER):
                    p = (q + WR) % PER
                    j = i + (q + WR) // PER
                    user = slot_user(p) + PER * j
                    sp.wait_ge(dn_hi_made, user + 1)
                    sp.wait_ge(dn_lo_made, user + 1)
                    sp.dma_start(raw[p % WR][:, :], w_moe[bass.ds(i * PER + (q + WR), 1)].rearrange("o p n -> (o p) n"))\
                      .then_inc(raw_in[p % WR], 16)
                    for e in range(EPER):
                        last_tile = ((e + 1) * FE - 1) // P
                        if q == min(last_tile + 1, PER - 1) and not last:
                            sp.wait_ge(af_made, (i * PER + last_tile + 1) * 2)
                            sp.dma_start(cw_b[e][:, :], scratch[bass.ds(i * EPER + (EPER + e), 1)]
                                         .rearrange("o t -> (o t)").partition_broadcast(P)).then_inc(cwb_in[e], 16)

            with sp.Fori(0, ITER - 1) as i:
                load_round(i, False)
            load_round(ITER - 1, True)
            for idx in range(2 * KT):
                dt, half = idx // 2, idx % 2
                sp.wait_ge(y_added, 3 * 2 * KT * ITER - 2 * KT + idx + 1)
                sp.dma_start(out_t[dt, :, half * NH:(half + 1) * NH], y_sum[:, dt, half * NH:(half + 1) * NH])\
                  .then_inc(out_written, 16)
            sp.wait_ge(out_written, 16 * 2 * KT)

        @block.gpsimd
        def _(pool):
            pool.dma_start(xres[:, :], x[0]).then_inc(xres_in, 16)
            nc.gpsimd.memset(minus_half[:, :], -0.5).then_inc(consts, 1)
            nc.gpsimd.memset(rms_eps[:, :], RMS_EPS).then_inc(consts, 1)
            nc.gpsimd.memset(ln_eps[:, :], LN_EPS).then_inc(consts, 1)
            for i in range(2):
                nc.gpsimd.memset(q_blk[i][:, :, :], 0.0).then_inc(consts, 1)
                nc.gpsimd.memset(v_ext[i][:, :, :, :], 1.0).then_inc(consts, 1)
            nc.gpsimd.memset(sc_ext[:, E:E + 1], -1.0).then_inc(consts, 1)
            nc.gpsimd.memset(sc_ext[:, E + 1:E + 2], -2.0).then_inc(consts, 1)
            nc.gpsimd.memset(top_s[:, TOP_K:TOP_K + 1], -1.0).then_inc(consts, 1)
            nc.gpsimd.memset(top_s[:, TOP_K + 1:8], -2.0).then_inc(consts, 1)
            pool.wait_ge(consts, 3)

            def norm_scale(n, i):
                rows = ITEM[i][1]
                pool.wait_ge(ss_made, KQ * n + (i + 1))
                nc.gpsimd.tensor_tensor(ms[0:rows, :], ss[0:rows, i % 2, :], rms_eps[0:rows, :], ALU.add).then_inc(ms_made, 1)
                pool.wait_ge(ms_made, KQ * n + (i + 1))
                wait(pool, kn_made, KQ * n + (i - 1))
                nc.gpsimd.tensor_tensor(rinv[0:rows, i % 2, :], ms[0:rows, :], minus_half[0:rows, :],
                                        ALU.pow).then_inc(rinv_made, 1)

            def layer_scale(t, mv, out, var_made, stat_made, scale_made):
                pool.wait_ge(stat_made, (t + 1) * 2)
                nc.gpsimd.tensor_tensor(out[:, 0:1], mv[:, 1:2], ln_eps[0:N, :], ALU.add).then_inc(var_made, 1)
                pool.wait_ge(var_made, t + 1)
                nc.gpsimd.tensor_tensor(out[:, 1:2], out[:, 0:1], minus_half[0:N, 0:1], ALU.pow).then_inc(scale_made, 1)

            def one(b, par, n, c):
                if c is not None:
                    layer_scale(c, mv_h, rstd_hb, var_h, bn_h, rstd_h)
                    pool.wait_ge(x1_made, c + 1)
                    nc.gpsimd.dma_start(xres[:, :], x[bass.ds(c + 1, 1)].rearrange("o t d -> (o t) d")).then_inc(xres_in, 16)
                if n is not None:
                    norm_scale(n, 0)
                    layer_scale(n, mv_x, rstd_xb, var_x, bn_x, rstd_x)
                    for i in (1, 2, 3):
                        norm_scale(n, i)

            batches(pool, one)
            layer_scale(B - 1, mv_h, rstd_hb, var_h, bn_h, rstd_h)

        @block.scalar
        def _(act):
            def split_w(j):
                act.wait_ge(w_in[j], 16)
                nc.scalar.activation(w_parts[0][:, j, :, :], w_raw[:, j, :, :], ACT.Copy).then_inc(w_hi_made, 1)

            def exps(b, j):
                rows = MT[j % 3][1]
                act.wait_ge(scores_done, b * UNITS + (j + 1))
                wait(act, pv_done, b * UNITS + (j - 1))
                nc.scalar.activation(probs[j % 2][0:rows, :].rearrange("p (a t) -> p a t", a=2),
                                     s_bank[0:rows, :, 0:4 * N], ACT.Exp, scale=float(HD) ** -0.5).then_inc(probs_made, 1)

            def squares(n, i):
                rows = ITEM[i][1]
                act.wait_ge(kq_done, KQ * n + (i + 1))
                wait(act, ss_made, KQ * n + i)
                nc.scalar.activation(sq[0:rows, :], kq_bank[0:rows, i % 2, :], ACT.Square,
                                     scale=float(HD) ** -0.5).then_inc(sq_made, 1)

            def part_hi(n, i):
                step, rows = ITEM[i]
                act.wait_ge(kn_made, KQ * n + (i + 1))
                wait(act, tr_done, parts_free(n, i))
                src = kn[0:rows, :].rearrange("p (h d) -> p h d", d=HD).unsqueeze(2).broadcast_to([rows, H, 2, HD])
                dst = stack4[i % 2][0:rows, :, 0:4:2, :] if step else stack4[i % 2][0:rows, :, 0:2, :]
                nc.scalar.activation(dst, src, ACT.Copy).then_inc(p_hi_made, 1)

            def copy_v(n, mt, par):
                rows = MT[mt][1]
                act.wait_ge(v_done, n * 3 + (mt + 1))
                wait(act, pv_done, (n - 1) * UNITS)
                if isinstance(n, int):
                    act.wait_ge(consts, 7)
                nc.scalar.activation(v_ext[par][0:rows, mt, :, 0:HD], v_bank[0:rows, :].rearrange("p (h d) -> p h d", d=HD),
                                     ACT.Copy).then_inc(v_copied, 1)

            def q_block(n, r, par):
                act.wait_ge(tr_done, n * TR + (6 + r))
                wait(act, scores_done, (n - 1) * UNITS)
                src = tr_bank[:, :].rearrange("p (a t) -> p a t", a=8)
                for h in range(2):
                    last = nc.scalar.activation(q_blk[par][64 * h:64 * h + 64, 8 * r:8 * r + 8, h * N:(h + 1) * N],
                                                src[64 * h:64 * h + 64, :, 0:N], ACT.Copy)
                last.then_inc(tr_used, 1)

            def one(b, par, n, c):
                q = 1 - par
                for j in range(UNITS):
                    if b is not None:
                        exps(b, j)
                    if n is not None:
                        if j == 0:
                            if isinstance(n, int) and n == 0:
                                split_w(0)
                            act.wait_ge(ctx_in, (n + 1) * 16)
                            wait(act, kq_done, n * KQ)
                            wait(act, v_done, n * 3)
                            nc.scalar.activation(c_parts[0][:, :, :], c_raw[:, :, :], ACT.Copy).then_inc(c_hi_made, 1)
                            if isinstance(n, int) and n == 0:
                                split_w(1)
                        if j == 1:
                            squares(n, 0)
                        if j == 2:
                            part_hi(n, 0)
                            copy_v(n, 0, q)
                            if isinstance(n, int) and n == 0:
                                split_w(2)
                        if j == 3:
                            squares(n, 1)
                        if j == 4:
                            part_hi(n, 1)
                            copy_v(n, 1, q)
                            act.wait_ge(xt_made, n + 1)
                            wait(act, kq_done, n * KQ - 1)
                            nc.scalar.activation(x_parts[0][:, :, :], xt[:, :, :], ACT.Copy).then_inc(x_hi_made, 1)
                        if j == 5:
                            squares(n, 2)
                        if j == 6:
                            part_hi(n, 2)
                            squares(n, 3)
                        if j == 7:
                            part_hi(n, 3)
                            copy_v(n, 2, q)
                            q_block(n, 0, q)
                        if j == 8:
                            q_block(n, 1, q)
                    if c is not None:
                        tail(c, j)

            def tail(c, j):
                if j == 4:
                    act.wait_ge(ht_made, c + 1)
                    nc.scalar.activation(h_parts[0][:, :, bass.ds(c * N, N)], ht[:, :, :], ACT.Copy).then_inc(h_hi_made, 1)
                if j == 7:
                    act.wait_ge(negm_made, c + 1)
                    nc.scalar.activation(pexp[:, :], lg[:, :], ACT.Exp, bias=neg_m[:, :],
                                         accum_out=pinv[:, 0:1]).then_inc(pexp_made, 1)

            batches(act, one)

            def split_gu(i, p):
                act.wait_ge(raw_in[p % WR], loads(i, p) * 16)
                nc.scalar.activation(gu_parts[p % WR][0][:, :, :, :].rearrange("p a k f -> p (a k f)"),
                                     raw[p % WR][:, 0:2 * D], ACT.Copy).then_inc(gu_hi_made, 1)

            split_gu(0, 0)
            split_gu(0, 1)
            for j in range(UNITS):
                tail(B - 1, j)
            act.wait_ge(cw_made, B)

            def silu(t, half):
                act.wait_ge(g_done, t * 2 + (half + 1))
                wait(act, gu_mult, t * 2 + (half - 1))
                nc.scalar.activation(act_g[half][:, :], g_bank[:, half, 0:NH], ACT.Silu).then_inc(silu_made, 1)

            def tile(i, p):
                t = i * PER + p
                if p + 2 < PER or not isinstance(i, int) or i < ITER - 1:
                    split_gu(i + (p + 2) // PER, (p + 2) % PER)
                for half in range(2):
                    silu(t, half)
                    act.wait_ge(af_made, t * 2 + (half + 1))
                    nc.scalar.activation(a_parts[HSLOT[p]][0][:, half * NH:(half + 1) * NH], act_f[half][:, :],
                                         ACT.Copy).then_inc(a_hi_made, 1)
                nc.scalar.activation(dn_parts[HSLOT[p]][0][:, :], raw[p % WR][:, 2 * D:3 * D], ACT.Copy).then_inc(dn_hi_made, 1)

            hidden_tiles(act, tile, lambda i, g: None)

        @block.vector
        def _(dve):
            def split_w(j):
                dve.wait_ge(w_hi_made, j + 1)
                nc.vector.tensor_tensor(w_parts[1][:, j, :, :], w_raw[:, j, :, :], w_parts[0][:, j, :, :].bitcast(F32),
                                        ALU.subtract).then_inc(w_lo_made, 1)

            def sums(n, i):
                rows = ITEM[i][1]
                dve.wait_ge(sq_made, KQ * n + (i + 1))
                wait(dve, ms_made, KQ * n + (i - 1))
                nc.vector.tensor_reduce(ss[0:rows, i % 2, :], sq[0:rows, :].rearrange("p (h d) -> p h d", d=HD),
                                        AX.X, ALU.add).then_inc(ss_made, 1)

            def normed(n, i):
                step, rows = ITEM[i]
                dve.wait_ge(rinv_made, KQ * n + (i + 1))
                wait(dve, p_hi_made, KQ * n + i)
                scale = rinv[0:rows, i % 2, :].unsqueeze(2).broadcast_to([rows, H, HD])
                nc.vector.tensor_tensor(kn[0:rows, :].rearrange("p (h d) -> p h d", d=HD),
                                        kq_bank[0:rows, i % 2, :].rearrange("p (h d) -> p h d", d=HD),
                                        scale, ALU.mult).then_inc(kn_made, 1)
                dve.wait_ge(p_hi_made, KQ * n + (i + 1))
                src = kn[0:rows, :].rearrange("p (h d) -> p h d", d=HD).unsqueeze(2).broadcast_to([rows, H, 2, HD])
                hi = stack4[i % 2][0:rows, :, 0:4:2, :] if step else stack4[i % 2][0:rows, :, 0:2, :]
                lo = stack4[i % 2][0:rows, :, 1:4:2, :] if step else stack4[i % 2][0:rows, :, 2:4, :]
                nc.vector.tensor_tensor(lo, src, hi, ALU.subtract).then_inc(p_lo_made, 1)

            def k_block(n, mt, r, par, which):
                r0, rows = MT[mt]
                dve.wait_ge(tr_done, n * TR + which)
                wait(dve, scores_done, (n - 1) * UNITS)
                nc.vector.tensor_copy(k_t[par][:, 8 * r:8 * r + 8, r0:r0 + rows],
                                      tr_bank[:, :].rearrange("p (a t) -> p a t", a=8)[:, :, 0:rows]).then_inc(tr_used, 1)

            def o_norm(b, g, par):
                dve.wait_ge(pv_done, b * UNITS + 3 * (g + 1))
                acc = o_bank[0:N, g % 2, 0:GH * HV].rearrange("p (h v) -> p h v", v=HV)
                wait(dve, o_normed, b * HG + (g - 1))
                nc.vector.reciprocal(o_inv[:, g % 2, :].unsqueeze(2), acc[:, :, HD:HV]).then_inc(o_inv_made, 1)
                dve.wait_ge(o_inv_made, b * HG + (g + 1))
                nc.vector.tensor_tensor(x1[par][:, g * GH * HD:(g + 1) * GH * HD].rearrange("p (h d) -> p h d", d=HD),
                                        acc[:, :, 0:HD], o_inv[:, g % 2, :].unsqueeze(2).broadcast_to([N, GH, HD]),
                                        ALU.mult).then_inc(o_normed, 1)

            def layer_stats(t, src, stats, mv, made):
                nc.vector.bn_stats(stats[:, :], src).then_inc(made, 1)
                dve.wait_ge(made, t * 2 + 1)
                carry_wait()
                nc.vector.bn_aggr(mv[:, :], stats[:, :]).then_inc(made, 1)

            def one(b, par, n, c):
                q = 1 - par
                for j in range(UNITS):
                    if c is not None and j < 3:
                        tail(c, j, q)
                    if b is not None and j in (4, 7, 10):
                        o_norm(b, j // 3 - 1, par)
                    if n is not None:
                        prepare(n, j, q)
                    if c is not None and j >= 3:
                        tail(c, j, q)

            def prepare(n, j, q):
                if j == 0:
                    if isinstance(n, int) and n == 0:
                        split_w(0)
                    dve.wait_ge(c_hi_made, n + 1)
                    nc.vector.tensor_tensor(c_parts[1][:, :, :], c_raw[:, :, :], c_parts[0][:, :, :].bitcast(F32),
                                            ALU.subtract).then_inc(c_lo_made, 1)
                    if isinstance(n, int) and n == 0:
                        split_w(1)
                if j == 1:
                    sums(n, 0)
                    dve.wait_ge(x_in, (n + 1) * 16)
                    layer_stats(n, xin[:, :], stats_x, mv_x, bn_x)
                if j == 2:
                    normed(n, 0)
                    dve.wait_ge(rstd_x, n + 1)
                    wait(dve, tr_done, (n - 1) * TR + 3)
                    nc.vector.tensor_scalar(xn[:, :], xin[:, :], mv_x[:, 0:1], rstd_xb[:, 1:2],
                                            ALU.subtract, ALU.mult).then_inc(xn_made, 1)
                    if isinstance(n, int) and n == 0:
                        split_w(2)
                        dve.wait_ge(eye_in, 16)
                        nc.vector.tensor_copy(id16[:, :], id32[:, :]).then_inc(id16_made, 1)
                if j == 3:
                    k_block(n, 0, 0, q, 1)
                    sums(n, 1)
                if j == 4:
                    normed(n, 1)
                    k_block(n, 0, 1, q, 2)
                    dve.wait_ge(tr_done, n * TR + 3)
                    wait(dve, x_hi_made, n)
                    nc.vector.tensor_copy(xt[:, :, :].rearrange("p k t -> p (k t)"),
                                          tr_bank[:, :].bitcast(F32)[:, 0:KT * N]).then_inc(xt_made, 1)
                    dve.wait_ge(x_hi_made, n + 1)
                    nc.vector.tensor_tensor(x_parts[1][:, :, :], xt[:, :, :], x_parts[0][:, :, :].bitcast(F32),
                                            ALU.subtract).then_inc(x_lo_made, 1)
                if j == 5:
                    k_block(n, 1, 0, q, 4)
                    sums(n, 2)
                if j == 6:
                    normed(n, 2)
                    k_block(n, 1, 1, q, 5)
                    sums(n, 3)
                if j == 7:
                    normed(n, 3)
                if j == 9:
                    k_block(n, 2, 0, q, 8)
                if j == 10:
                    k_block(n, 2, 1, q, 9)

            def tail(c, j, par):
                if j == 0:
                    o_norm(c, 3, par)
                    dve.wait_ge(xres_in, (c + 1) * 16)
                    dve.wait_ge(o_normed, (c + 1) * HG)
                    nc.vector.tensor_tensor(x1[par][:, :], x1[par][:, :], xres[:, :], ALU.add).then_inc(x1_made, 1)
                    dve.wait_ge(x1_made, c + 1)
                    layer_stats(c, x1[par][:, :], stats_h, mv_h, bn_h)
                if j == 1:
                    dve.wait_ge(rstd_h, c + 1)
                    nc.vector.tensor_scalar(hn[:, :], x1[par][:, :], mv_h[:, 0:1], rstd_hb[:, 1:2],
                                            ALU.subtract, ALU.mult).then_inc(hn_made, 1)
                if j == 3:
                    dve.wait_ge(ht_done, c + 1)
                    nc.vector.tensor_copy(ht[:, :, :].rearrange("p k t -> p (k t)"), v_bank[:, 0:KT * N]).then_inc(ht_made, 1)
                if j == 4:
                    dve.wait_ge(h_hi_made, c + 1)
                    nc.vector.tensor_tensor(h_parts[1][:, :, bass.ds(c * N, N)], ht[:, :, :],
                                            h_parts[0][:, :, bass.ds(c * N, N)].bitcast(F32), ALU.subtract).then_inc(h_lo_made, 1)
                if j == 5:
                    dve.wait_ge(x1t_done, c + 1)
                    nc.vector.tensor_copy(y_sum[:, :, bass.ds(c * N, N)],
                                          v_bank[:, 0:KT * N].rearrange("p (k t) -> p k t", k=KT)).then_inc(x1t_made, 1)
                if j == 6:
                    dve.wait_ge(lg_done, c + 1)
                    nc.vector.tensor_copy(lg[:, :], v_bank[0:N, 0:E]).then_inc(lg_made, 1)
                    dve.wait_ge(lg_made, c + 1)
                    carry_wait()
                    nc.vector.max(top_l[:, :], lg[:, :]).then_inc(gate_step, 1)
                    dve.wait_ge(gate_step, c * 5 + 1)
                    nc.vector.tensor_scalar(neg_m[:, :], top_l[:, 0:1], -1.0, None, ALU.mult).then_inc(negm_made, 1)
                if j == 7:
                    dve.wait_ge(pexp_made, c + 1)
                    nc.vector.reciprocal(pinv[:, 1:2], pinv[:, 0:1]).then_inc(gate_step, 1)
                    dve.wait_ge(gate_step, c * 5 + 2)
                    nc.vector.tensor_scalar(sc_ext[:, 0:E], pexp[:, :], pinv[:, 1:2], None, ALU.mult).then_inc(gate_step, 1)
                    dve.wait_ge(gate_step, c * 5 + 3)
                    dve.wait_ge(consts, 11)
                    carry_wait()
                    nc.vector.max(top_l[:, :], sc_ext[:, 0:E]).then_inc(gate_step, 1)
                    dve.wait_ge(gate_step, c * 5 + 4)
                    nc.vector.tensor_copy(top_s[:, 0:TOP_K], top_l[:, 0:TOP_K]).then_inc(gate_step, 1)
                    dve.wait_ge(gate_step, c * 5 + 5)
                    carry_wait()
                    nc.vector.match_replace(rest[:, :], top_s[:, :], sc_ext[:, :], 0.0).then_inc(rest_made, 1)
                    dve.wait_ge(rest_made, c + 1)
                    nc.vector.tensor_tensor(cw[:, :], sc_ext[:, 0:E], rest[:, 0:E], ALU.subtract).then_inc(cw_made, 1)
                if j == 8:
                    dve.wait_ge(cwt_done, c + 1)
                    nc.vector.tensor_copy(cw_t[:, bass.ds(c * N, N)], v_bank[0:E, 0:N]).then_inc(cwt_made, 1)

            batches(dve, one)

            def split_gu(i, p):
                dve.wait_ge(gu_hi_made, i * PER + (p + 1))
                nc.vector.tensor_tensor(gu_parts[p % WR][1][:, :, :, :].rearrange("p a k f -> p (a k f)"), raw[p % WR][:, 0:2 * D],
                                        gu_parts[p % WR][0][:, :, :, :].rearrange("p a k f -> p (a k f)").bitcast(F32),
                                        ALU.subtract).then_inc(gu_lo_made, 1)

            split_gu(0, 0)
            split_gu(0, 1)
            for j in range(UNITS):
                tail(B - 1, j, 1)

            def tile(i, p):
                t = i * PER + p
                if p + 2 < PER or not isinstance(i, int) or i < ITER - 1:
                    split_gu(i + (p + 2) // PER, (p + 2) % PER)
                for half in range(2):
                    k = t * 2 + (half + 1)
                    cols = slice(half * NH, (half + 1) * NH)
                    dve.wait_ge(silu_made, k)
                    dve.wait_ge(u_done, k)
                    nc.vector.tensor_tensor(act_u[half][:, :], act_g[half][:, :], u_bank[:, half, 0:NH], ALU.mult).then_inc(gu_mult, 1)
                    dve.wait_ge(gu_mult, k)
                    wait(dve, a_hi_made, k - 2)
                    segments = cw_segments(p)
                    for n, (r0, r1, e) in enumerate(segments):
                        dve.wait_ge(cwb_in[e], (i + 1) * 16)
                        last = nc.vector.tensor_tensor(act_f[half][r0:r1, :], act_u[half][r0:r1, :], cw_b[e][r0:r1, cols], ALU.mult)
                    last.then_inc(af_made, 1)
                    dve.wait_ge(a_hi_made, k)
                    a = a_parts[HSLOT[p]]
                    nc.vector.tensor_tensor(a[1][:, cols], act_f[half][:, :], a[0][:, cols].bitcast(F32),
                                            ALU.subtract).then_inc(a_lo_made, 1)
                dve.wait_ge(dn_hi_made, t + 1)
                d = dn_parts[HSLOT[p]]
                nc.vector.tensor_tensor(d[1][:, :], raw[p % WR][:, 2 * D:3 * D], d[0][:, :].bitcast(F32),
                                        ALU.subtract).then_inc(dn_lo_made, 1)

            def add_group(i, g):
                for idx in range(2 * KT):
                    dt, half = idx // 2, idx % 2
                    k = i * (6 * KT) + (2 * KT * g + idx + 1)
                    dve.wait_ge(y_done, k)
                    y = y_sum[:, dt, half * NH:(half + 1) * NH]
                    nc.vector.tensor_tensor(y, y, y_bank[:, idx % 4, 0:NH], ALU.add).then_inc(y_added, 1)

            hidden_tiles(dve, tile, add_group)

        @block.tensor
        def _(pe):
            def project(out, rows, lhs, w, col):
                for k in range(KT):
                    for s, (a, b) in enumerate(CASES):
                        last = nc.tensor.matmul(out, lhs[a][:, k, col:col + rows], w_parts[b][:, w, k, :],
                                                start=(k == 0 and s == 0), stop=(k == KT - 1 and s == 2))
                return last

            def project_k(n, mt, i):
                if mt == 0:
                    pe.wait_ge(c_hi_made, n + 1)
                    pe.wait_ge(c_lo_made, n + 1)
                    pe.wait_ge(w_lo_made, 1)
                wait(pe, kn_made, KQ * n + (i - 1))
                project(kq_bank[0:MT[mt][1], i % 2, :], MT[mt][1], c_parts, 0, MT[mt][0]).then_inc(kq_done, 1)

            def project_q(n):
                pe.wait_ge(x_hi_made, n + 1)
                pe.wait_ge(x_lo_made, n + 1)
                pe.wait_ge(w_lo_made, 3)
                wait(pe, kn_made, KQ * n + 1)
                project(kq_bank[0:N, 0, :], N, x_parts, 2, 0).then_inc(kq_done, 1)

            def project_v(n, mt):
                pe.wait_ge(w_lo_made, 2)
                project(v_bank[0:MT[mt][1], :], MT[mt][1], c_parts, 1, MT[mt][0]).then_inc(v_done, 1)

            def bank_free(n, which):
                wait(pe, tr_used, n * (TR - 1) + (which if which < 3 else which - 1))
                wait(pe, xt_made, n + (1 if which >= 3 else 0))

            def stack_transposes(n, i, r, which):
                rows = ITEM[i][1]
                pe.wait_ge(id16_made, 1)
                pe.wait_ge(p_lo_made, KQ * n + (i + 1))
                bank_free(n, which)
                for a in range(8):
                    pair = stack4[i % 2][0:rows, 2 * (8 * r + a):2 * (8 * r + a) + 2, :, :].rearrange("p h s d -> p (h s d)")
                    last = nc.tensor.transpose(tr_bank[:, a * P:a * P + rows], pair, id16[0:rows, 0:rows])
                last.then_inc(tr_done, 1)

            def scores(b, j, par):
                g, mt = j // 3, j % 3
                r0, rows = MT[mt]
                wait(pe, probs_made, b * UNITS + j)
                if j == 0:
                    pe.wait_ge(tr_used, (b + 1) * (TR - 1))
                    pe.wait_ge(xt_made, b + 1)
                for a in range(4):
                    last = nc.tensor.matmul(s_bank[0:rows, a // 2, (a % 2) * 2 * N:(a % 2 + 1) * 2 * N],
                                            k_t[par][:, 4 * g + a, r0:r0 + rows], q_blk[par][:, 4 * g + a, :],
                                            start=True, stop=True)
                last.then_inc(scores_done, 1)

            def values(b, j, par):
                g, mt = j // 3, j % 3
                rows = MT[mt][1]
                pe.wait_ge(probs_made, b * UNITS + (j + 1))
                if j == 0:
                    pe.wait_ge(v_copied, (b + 1) * 3)
                if mt == 0:
                    wait(pe, o_normed, b * HG + (g - 1))
                for h in range(GH):
                    last = nc.tensor.matmul(o_bank[0:N, g % 2, h * HV:(h + 1) * HV], probs[j % 2][0:rows, h * N:(h + 1) * N],
                                            v_ext[par][0:rows, mt, g * GH + h, :], start=(mt == 0 and h == 0), stop=(mt == 2),
                                            skip_group_check=True)
                last.then_inc(pv_done, 1)

            def one(b, par, n, c):
                q = 1 - par
                for j in range(UNITS):
                    if b is not None:
                        scores(b, j, par)
                    if c is not None and j == 0:
                        values(c, UNITS - 1, q)
                    if n is not None:
                        if j == 1:
                            project_k(n, 0, 0)
                        if j == 2:
                            wait(pe, v_copied, n * 3)
                            if c is not None:
                                pe.wait_ge(x1_made, c + 1)
                            project_v(n, 0)
                        if j == 3:
                            stack_transposes(n, 0, 0, 0)
                            project_k(n, 1, 1)
                            pe.wait_ge(v_copied, n * 3 + 1)
                    if c is not None:
                        tail_early(c, j, q)
                    if n is not None:
                        if j == 4:
                            stack_transposes(n, 0, 1, 1)
                            if c is not None:
                                pe.wait_ge(ht_made, c + 1)
                            else:
                                pe.wait_ge(v_copied, n * 3 + 1)
                            project_v(n, 1)
                            pe.wait_ge(xn_made, n + 1)
                            bank_free(n, 2)
                            for k in range(KT):
                                last = nc.tensor.transpose(tr_bank[:, :].bitcast(F32)[:, k * N:(k + 1) * N],
                                                           xn[:, k * P:(k + 1) * P], id32[0:N, 0:N])
                            last.then_inc(tr_done, 1)
                        if j == 5:
                            stack_transposes(n, 1, 0, 3)
                            project_q(n)
                            pe.wait_ge(v_copied, n * 3 + 2)
                        if j == 6:
                            stack_transposes(n, 1, 1, 4)
                            project_k(n, 2, 3)
                    if c is not None:
                        tail_late(c, j, q)
                    if n is not None:
                        if j == 7:
                            stack_transposes(n, 2, 0, 5)
                            if c is not None:
                                pe.wait_ge(lg_made, c + 1)
                            project_v(n, 2)
                        if j == 8:
                            stack_transposes(n, 2, 1, 6)
                            pe.wait_ge(v_copied, n * 3 + 3)
                        if j == 9:
                            stack_transposes(n, 3, 0, 7)
                        if j == 10:
                            stack_transposes(n, 3, 1, 8)
                    if c is not None:
                        tail_last(c, j)
                    if b is not None and j > 0:
                        values(b, j - 1, par)

            def tail_early(c, j, par):
                if j == 3:
                    pe.wait_ge(hn_made, c + 1)
                    pe.wait_ge(eye_in, 16)
                    for k in range(KT):
                        last = nc.tensor.transpose(v_bank[:, k * N:(k + 1) * N], hn[:, k * P:(k + 1) * P], id32[0:N, 0:N])
                    last.then_inc(ht_done, 1)

            def tail_late(c, j, par):
                if j == 5:
                    pe.wait_ge(ht_made, c + 1)
                    for k in range(KT):
                        last = nc.tensor.transpose(v_bank[:, k * N:(k + 1) * N], x1[par][:, k * P:(k + 1) * P], id32[0:N, 0:N])
                    last.then_inc(x1t_done, 1)
                if j == 6:
                    pe.wait_ge(x1t_made, c + 1)
                    pe.wait_ge(gate_in, 16)
                    for k in range(KT):
                        last = nc.tensor.matmul(v_bank[0:N, 0:E], ht[:, k, :], gate_w[:, k, :], start=(k == 0), stop=(k == KT - 1))
                    last.then_inc(lg_done, 1)

            def tail_last(c, j):
                if j == 8:
                    pe.wait_ge(lg_made, c + 1)
                    pe.wait_ge(cw_made, c + 1)
                    nc.tensor.transpose(v_bank[0:E, 0:N], cw[:, :], id32[0:N, 0:N]).then_inc(cwt_done, 1)

            batches(pe, one)
            values(B - 1, UNITS - 1, 1)
            for j in range(UNITS):
                tail_early(B - 1, j, 1)
                tail_late(B - 1, j, 1)
            pe.wait_ge(h_hi_made, B)
            pe.wait_ge(h_lo_made, B)

            def gate_up(i, p, half):
                t = i * PER + p
                pe.wait_ge(gu_lo_made, t + 1)
                w = gu_parts[p % WR]
                for s, (bank, freed, done) in enumerate(((g_bank, silu_made, g_done), (u_bank, gu_mult, u_done))):
                    wait(pe, freed, t * 2 + (half - 1))
                    for k in range(KT):
                        for m, (a, b) in enumerate(CASES):
                            last = nc.tensor.matmul(bank[:, half, 0:NH], w[a][:, s, k, :], h_parts[b][:, k, half * NH:(half + 1) * NH],
                                                    start=(k == 0 and m == 0), stop=(k == KT - 1 and m == 2))
                    last.then_inc(done, 1)

            def tile(i, p):
                gate_up(i, p, 0)
                if isinstance(i, int) and i == 0 and p == 0:
                    tail_last(B - 1, 8)
                gate_up(i, p, 1)

            def down(i, g):
                first, end = GROUPS[g]
                t_end = i * PER + end
                pe.wait_ge(a_lo_made, t_end * 2)
                pe.wait_ge(dn_lo_made, t_end)
                for idx in range(2 * KT):
                    dt, half = idx // 2, idx % 2
                    if idx >= 4:
                        pe.wait_ge(y_added, i * (6 * KT) + (2 * KT * g + idx - 3))
                    for p in range(first, end):
                        for m, (a, b) in enumerate(CASES):
                            last = nc.tensor.matmul(y_bank[:, idx % 4, 0:NH], dn_parts[HSLOT[p]][a][:, dt * P:(dt + 1) * P],
                                                    a_parts[HSLOT[p]][b][:, half * NH:(half + 1) * NH],
                                                    start=(p == first and m == 0), stop=(p == end - 1 and m == 2))
                    last.then_inc(y_done, 1)

            hidden_tiles(pe, tile, down)


def kernel(x, ctx_2048, L0_xattn_Wq, L0_xattn_Wk, L0_xattn_Wv, L0_ffn_gate_w, L0_ffn_w_gate, L0_ffn_w_up, L0_ffn_w_down):
    import concourse.bacc as bacc
    import numpy as np
    from concourse.bass_utils import run_bass_kernel_spmd

    B, N, D = x.shape
    M = ctx_2048.shape[1]
    E, F, _ = L0_ffn_w_gate.shape
    KT, TILES = D // P, E * F // P

    def k_major(w):
        return np.asarray(w).T.reshape(KT, P, -1).transpose(1, 0, 2)

    kv = np.concatenate([np.asarray(L0_xattn_Wk), np.asarray(L0_xattn_Wv)], axis=0)
    w_kvq = np.stack([k_major(kv[0::2]), k_major(kv[1::2]), k_major(L0_xattn_Wq)], axis=1)
    ctx_t = np.asarray(ctx_2048).transpose(0, 2, 1).reshape(B, KT, P, M).transpose(0, 2, 1, 3)

    def hidden_major(w):
        return np.asarray(w).reshape(TILES, P, KT, P).transpose(0, 3, 2, 1).reshape(TILES, P, KT * P)

    down = np.asarray(L0_ffn_w_down).transpose(0, 2, 1).reshape(TILES, P, D)
    w_moe = np.concatenate([hidden_major(L0_ffn_w_gate), hidden_major(L0_ffn_w_up), down], axis=2)

    ins = {
        "x": np.asarray(x), "ctx_t": ctx_t, "w_kvq": w_kvq, "gate_t": k_major(L0_ffn_gate_w), "w_moe": w_moe,
        "eye": np.eye(P, dtype=np.float32),
    }
    ins = {f"in_{name}": np.ascontiguousarray(a) for name, a in ins.items()}
    nc = bacc.Bacc("TRN2", target_bir_lowering=False, num_devices=1)
    aps = [nc.dram_tensor(name, a.shape, mybir.dt.from_np(a.dtype), kind="ExternalInput").ap() for name, a in ins.items()]
    out = nc.dram_tensor("out_t", (KT, P, B * N), F32, kind="ExternalOutput").ap()
    xattn_moe_program(nc, *aps, out)
    r = run_bass_kernel_spmd(nc, [ins], core_ids=[0])
    return r.results[0]["out_t"].reshape(D, B * N).T.reshape(B, N, D)
```

```python
import math
from contextlib import ExitStack

import concourse.bass as bass
from concourse import mybir

F32 = mybir.dt.float32
F32R = mybir.dt.float32r
F16 = mybir.dt.float16
ALU = mybir.AluOpType
ACT = mybir.ActivationFunctionType
AX = mybir.AxisListType

P = 128
LN_EPS = 1e-5
RMS_EPS = 1e-6
TOP_K = 6
GUESS_SCALE = -0.5 * math.log(2.0) / 2 ** 23
GUESS_BIAS = 0.5 * math.log(2.0) * (127 - 0.043)


def xattn_moe_program(nc, x, ctx_t, w_kvq, gate_t, w_moe, eye, out_t):
    B, N, D = x.shape
    _, _, KT, M = ctx_t.shape
    E = gate_t.shape[2]
    TILES = w_moe.shape[0]
    FE = TILES * P // E
    H = 32
    HD = D // H
    HV = HD + 1
    T = B * N
    NH = T // 2
    CT = 2 * P
    MT = [(0, P), (P, P), (2 * P, M - 2 * P)]
    PAIRS = H // 2
    HG = 4
    GH = H // HG
    UNITS = HG * len(MT)
    KQ = 4
    TR = 9
    PER = 11
    EPER = PER * P // FE
    ITER = TILES // PER
    assert PER * P == EPER * FE and ITER * PER == TILES and D == KT * P and T == 2 * NH
    GROUPS = [(0, 4), (4, 8), (8, 11)]
    HSLOT = [0, 1, 2, 3, 4, 5, 6, 7, 1, 2, 3]
    WR = 4
    CASES = [(0, 0), (0, 1), (1, 0)]

    scratch = nc.dram_tensor("combine_scratch", (E, T), F32, kind="Internal").ap()

    with ExitStack() as ctx:
        def sem(name):
            return ctx.enter_context(nc.semaphore(name))

        def tensors(stack):
            return (lambda name, shape, dt=F32: stack.enter_context(nc.sbuf_tensor(name, shape, dt)),
                    lambda name, shape, dt=F32: stack.enter_context(nc.psum_tensor(name, shape, dt)))

        staging = ExitStack()
        sb, _ = tensors(staging)
        w_raw = sb("w_raw", [P, 3, KT, D])
        staging.close()

        sb, _ = tensors(ctx)
        y_sum = sb("y_sum", [P, KT, T])
        h_parts = [sb("h_hi", [P, KT, T], F32R), sb("h_lo", [P, KT, T], F32R)]
        id32 = sb("id32", [P, P])
        id16 = sb("id16", [P, P], F16)
        gate_w = sb("gate_w", [P, KT, E])
        cw = sb("cw", [N, E])
        cw_t = sb("cw_t", [E, T])
        minus_half = sb("minus_half", [P, 1])
        guess_bias = sb("guess_bias", [P, 1])
        ln_eps = sb("ln_eps", [P, 1])
        carrier = sb("carrier", [1, 1])

        att = ExitStack()
        sb, ps = tensors(att)
        w_parts = [sb("w_hi", [P, 3, KT, D], F32R), sb("w_lo", [P, 3, KT, D], F32R)]
        c_raw = sb("c_raw", [P, KT, M])
        c_parts = [sb("c_hi", [P, KT, M], F32R), sb("c_lo", [P, KT, M], F32R)]
        xin = sb("xin", [N, D])
        xres = sb("xres", [N, D])
        xn = sb("xn", [N, D])
        xt = sb("xt", [P, KT, N])
        x_parts = [sb("xt_hi", [P, KT, N], F32R), sb("xt_lo", [P, KT, N], F32R)]
        stats_x, mv_x, rstd_xb = sb("stats_x", [N, 6]), sb("mv_x", [N, 2]), sb("rstd_xb", [N, 2])
        stats_h, mv_h, rstd_hb = sb("stats_h", [N, 6]), sb("mv_h", [N, 2]), sb("rstd_hb", [N, 2])
        k_raw = [sb(f"k_raw{i}", [P, D]) for i in range(KQ)]
        sq = [sb(f"sq{i}", [P, D]) for i in range(2)]
        ss = sb("ss", [P, KQ, H])
        ms, guess = sb("ms", [P, 2, H]), sb("guess", [P, 2, H])
        nt = [sb(f"nt{i}", [P, 2, H]) for i in range(4)]
        rinv = sb("rinv", [P, KQ, H])
        kn = [sb(f"kn{i}", [P, D]) for i in range(2)]
        stack4 = [sb(f"stack4_{i}", [P, H, 4, HD], F16) for i in range(2)]
        k_t = [sb(f"k_t{i}", [P, PAIRS, M], F16) for i in range(2)]
        q_blk = [sb(f"q_blk{i}", [P, PAIRS, 2 * N], F16) for i in range(2)]
        v_ext = [sb(f"v_ext{i}", [P, 3, H, HV]) for i in range(2)]
        probs = [sb(f"probs{i}", [P, GH * N]) for i in range(2)]
        o_inv = sb("o_inv", [N, 2, GH])
        x1 = [sb(f"x1_{i}", [N, D]) for i in range(2)]
        hn = sb("hn", [N, D])
        ht = sb("ht", [P, KT, N])
        lg = sb("lg", [N, E])
        top_l = sb("top_l", [N, 8])
        neg_m = sb("neg_m", [N, 1])
        pexp = sb("pexp", [N, E])
        pinv = sb("pinv", [N, 2])
        sc_ext = sb("sc_ext", [N, E + 2])
        top_s = sb("top_s", [N, 8])
        rest = sb("rest", [N, E + 2])
        s_bank = ps("s_bank", [P, 2, 512])
        kq_bank = ps("kq_bank", [P, 2, 512])
        o_bank = ps("o_bank", [P, 2, 512])
        tr_bank = ps("tr_bank", [P, 1024], F16)
        v_bank = ps("v_bank", [P, 512])
        att.close()

        sb, ps = tensors(ctx)
        raw_gu = [sb(f"raw_gu{i}", [P, 2 * D]) for i in range(WR)]
        raw_dn = [sb(f"raw_dn{i}", [P, D]) for i in range(WR)]
        gu_parts = [[sb(f"gu_hi{i}", [P, 2, KT, P], F32R), sb(f"gu_lo{i}", [P, 2, KT, P], F32R)] for i in range(WR)]
        dn_parts = [[sb(f"dn_hi{i}", [P, D], F32R), sb(f"dn_lo{i}", [P, D], F32R)] for i in range(8)]
        a_parts = [[sb(f"a_hi{i}", [P, T], F32R), sb(f"a_lo{i}", [P, T], F32R)] for i in range(8)]
        cw_b = [sb(f"cw_b{i}", [P, T]) for i in range(EPER)]
        act_g = [sb(f"act_g{i}", [P, NH]) for i in range(2)]
        act_u = [sb(f"act_u{i}", [P, NH]) for i in range(2)]
        act_f = [sb(f"act_f{i}", [P, NH]) for i in range(2)]
        g_bank = ps("g_bank", [P, 2, 512])
        u_bank = ps("u_bank", [P, 2, 512])
        y_bank = ps("y_bank", [P, 4, 512])

        eye_in, gate_in = sem("eye_in"), sem("gate_in")
        w_in = [sem(f"w_in{i}") for i in range(3)]
        ctx_in, x_in, xres_in = sem("ctx_in"), sem("x_in"), sem("xres_in")
        consts = sem("consts")
        id16_made = sem("id16_made")
        w_hi_made, w_lo_made = sem("w_hi_made"), sem("w_lo_made")
        c_hi_made, c_lo_made = sem("c_hi_made"), sem("c_lo_made")
        bn_x, var_x, rstd_x, xn_made = sem("bn_x"), sem("var_x"), sem("rstd_x"), sem("xn_made")
        xt_made, x_hi_made, x_lo_made = sem("xt_made"), sem("x_hi_made"), sem("x_lo_made")
        kq_done, v_done = sem("kq_done"), sem("v_done")
        sq_made, ss_made, raw_copied = sem("sq_made"), sem("ss_made"), sem("raw_copied")
        ms_made, guess_made, newton, rinv_made = sem("ms_made"), sem("guess_made"), sem("newton"), sem("rinv_made")
        kn_made, p_hi_made, p_lo_made = sem("kn_made"), sem("p_hi_made"), sem("p_lo_made")
        v_copied = sem("v_copied")
        tr_done, tr_used = sem("tr_done"), sem("tr_used")
        scores_done, probs_made, pv_done, o_normed = sem("scores_done"), sem("probs_made"), sem("pv_done"), sem("o_normed")
        o_inv_made, x1_made = sem("o_inv_made"), sem("x1_made")
        bn_h, var_h, rstd_h, hn_made = sem("bn_h"), sem("var_h"), sem("rstd_h"), sem("hn_made")
        ht_done, ht_made, h_hi_made, h_lo_made = sem("ht_done"), sem("ht_made"), sem("h_hi_made"), sem("h_lo_made")
        x1t_done, x1t_made = sem("x1t_done"), sem("x1t_made")
        lg_done, lg_made, negm_made, pexp_made = sem("lg_done"), sem("lg_made"), sem("negm_made"), sem("pexp_made")
        gate_step, cw_made, cwt_done, cwt_made = sem("gate_step"), sem("cw_made"), sem("cwt_done"), sem("cwt_made")
        rest_made = sem("rest_made")
        scratch_written = sem("scratch_written")
        gu_in = [sem(f"gu_in{i}") for i in range(WR)]
        dn_in = [sem(f"dn_in{i}") for i in range(WR)]
        cwb_in = [sem(f"cwb_in{i}") for i in range(EPER)]
        gu_hi_made, gu_lo_made, dn_hi_made, dn_lo_made = sem("gu_hi_made"), sem("gu_lo_made"), sem("dn_hi_made"), sem("dn_lo_made")
        g_done, u_done = sem("g_done"), sem("u_done")
        silu_made, gu_mult, af_made, a_hi_made, a_lo_made = sem("silu_made"), sem("gu_mult"), sem("af_made"), sem("a_hi_made"), sem("a_lo_made")
        y_done, y_added, out_written = sem("y_done"), sem("y_added"), sem("out_written")

        block = ctx.enter_context(nc.Block())

        def wait(eng, semaphore, value):
            if not isinstance(value, int) or value > 0:
                eng.wait_ge(semaphore, value)

        def carry_wait():
            nc.vector.memset(carrier[:, :], 0.0)

        def batches(eng, one):
            one(None, 1, 0, None, 1)
            one(0, 0, 1, None, 2)
            with eng.Fori(0, (B - 4) // 2) as i:
                one(i * 2 + 1, 1, i * 2 + 2, i * 2, i * 2 + 3)
                one(i * 2 + 2, 0, i * 2 + 3, i * 2 + 1, i * 2 + 4)
            one(B - 3, 1, B - 2, B - 4, B - 1)
            one(B - 2, 0, B - 1, B - 3, None)
            one(B - 1, 1, None, B - 2, None)

        def hidden_tiles(eng, one, group):
            def round_(i, more):
                for p in range(1, PER):
                    one(i, p)
                    if p == 4:
                        group(i, 0)
                    if p == 8:
                        group(i, 1)
                if more:
                    one(i + 1, 0)
                group(i, 2)
            one(0, 0)
            with eng.Fori(0, ITER - 1) as i:
                round_(i, True)
            round_(ITER - 1, False)

        ITEM = [(0, MT[0][1]), (0, MT[1][1]), (0, MT[2][1]), (1, N)]
        LAST_TR = [3, 5, 7, 9]

        def parts_free(n, item):
            return TR * n + LAST_TR[item - 2] - (TR if item < 2 else 0)

        def slot_user(p):
            return p - WR if p >= WR else max(q for q in range(PER) if q % WR == p % WR) - PER

        def loads(i, p):
            return i * len([q for q in range(PER) if q % WR == p % WR]) + p // WR + 1

        def cw_segments(p):
            cuts = {0, P} | {e * FE - p * P for e in range(EPER) if 0 < e * FE - p * P < P}
            if 32 in cuts:
                cuts.add(64)
            cuts = sorted(cuts)
            return [(a, b, (p * P + a) // FE) for a, b in zip(cuts, cuts[1:])]

        @block.sync
        def _(sp):
            sp.dma_start(w_raw[:, 0, :, :], w_kvq[:, 0, :, :]).then_inc(w_in[0], 16)
            sp.dma_start(c_raw[:, :, :], ctx_t[0]).then_inc(ctx_in, 16)
            for j in range(1, 3):
                sp.dma_start(w_raw[:, j, :, :], w_kvq[:, j, :, :]).then_inc(w_in[j], 16)
            sp.dma_start(id32[:, :], eye).then_inc(eye_in, 16)
            sp.dma_start(xin[:, :], x[0]).then_inc(x_in, 16)
            sp.dma_start(gate_w[:, :, :], gate_t).then_inc(gate_in, 16)
            with sp.Fori(1, B) as n:
                sp.wait_ge(c_hi_made, n * 2)
                sp.wait_ge(c_lo_made, n * 2)
                sp.dma_start(c_raw[:, :, :], ctx_t[bass.ds(n, 1)].rearrange("o p k m -> (o p) k m")).then_inc(ctx_in, 16)
                sp.wait_ge(xn_made, n)
                sp.dma_start(xin[:, :], x[bass.ds(n, 1)].rearrange("o t d -> (o t) d")).then_inc(x_in, 16)
            sp.wait_ge(kq_done, KQ * B)
            sp.wait_ge(v_done, 3 * B)
            for t in range(WR):
                sp.dma_start(raw_gu[t][:, :], w_moe[t, :, 0:2 * D]).then_inc(gu_in[t], 16)
            for t in range(WR):
                sp.dma_start(raw_dn[t][:, :], w_moe[t, :, 2 * D:3 * D]).then_inc(dn_in[t], 16)
            sp.wait_ge(cwt_made, B)
            sp.dma_start(scratch, cw_t[:, :]).then_inc(scratch_written, 16)
            sp.wait_ge(scratch_written, 16)
            for e in range(EPER):
                sp.dma_start(cw_b[e][:, :], scratch[e].partition_broadcast(P)).then_inc(cwb_in[e], 16)

            def load(i, q, ahead, ring, cols, sems, hi_made, lo_made):
                p = (q + ahead) % PER
                user = slot_user(p) + PER * (i + (q + ahead) // PER)
                sp.wait_ge(hi_made, user + 1)
                sp.wait_ge(lo_made, user + 1)
                sp.dma_start(ring[p % WR][:, :], w_moe[bass.ds(i * PER + (q + ahead), 1), :, cols].rearrange("o p n -> (o p) n"))\
                  .then_inc(sems[p % WR], 16)

            def load_round(i, last):
                for q in range(PER):
                    if not last or q + WR < PER:
                        load(i, q, WR, raw_gu, slice(0, 2 * D), gu_in, gu_hi_made, gu_lo_made)
                    if not last or q + WR < PER:
                        load(i, q, WR, raw_dn, slice(2 * D, 3 * D), dn_in, dn_hi_made, dn_lo_made)
                    for e in range(EPER):
                        last_tile = ((e + 1) * FE - 1) // P
                        if q == min(last_tile + 1, PER - 1) and not last:
                            sp.wait_ge(af_made, (i * PER + last_tile + 1) * 2)
                            sp.dma_start(cw_b[e][:, :], scratch[bass.ds(i * EPER + (EPER + e), 1)]
                                         .rearrange("o t -> (o t)").partition_broadcast(P)).then_inc(cwb_in[e], 16)

            with sp.Fori(0, ITER - 1) as i:
                load_round(i, False)
            load_round(ITER - 1, True)
            for idx in range(2 * KT):
                dt, half = idx // 2, idx % 2
                sp.wait_ge(y_added, 3 * 2 * KT * ITER - 2 * KT + idx + 1)
                sp.dma_start(out_t[dt, :, half * NH:(half + 1) * NH], y_sum[:, dt, half * NH:(half + 1) * NH])\
                  .then_inc(out_written, 16)
            sp.wait_ge(out_written, 16 * 2 * KT)

        @block.gpsimd
        def _(pool):
            pool.dma_start(xres[:, :], x[0]).then_inc(xres_in, 16)
            nc.gpsimd.memset(minus_half[:, :], -0.5).then_inc(consts, 1)
            nc.gpsimd.memset(guess_bias[:, :], GUESS_BIAS).then_inc(consts, 1)
            nc.gpsimd.memset(ln_eps[:, :], LN_EPS).then_inc(consts, 1)
            nc.gpsimd.memset(ss[:, :, :], 1.0).then_inc(consts, 1)
            for i in range(2):
                nc.gpsimd.memset(q_blk[i][:, :, :], 0.0).then_inc(consts, 1)
                nc.gpsimd.memset(v_ext[i][:, :, :, :], 1.0).then_inc(consts, 1)
            nc.gpsimd.memset(sc_ext[:, E:E + 1], -1.0).then_inc(consts, 1)
            nc.gpsimd.memset(sc_ext[:, E + 1:E + 2], -2.0).then_inc(consts, 1)
            nc.gpsimd.memset(top_s[:, TOP_K:TOP_K + 1], -1.0).then_inc(consts, 1)
            nc.gpsimd.memset(top_s[:, TOP_K + 1:8], -2.0).then_inc(consts, 1)
            pool.wait_ge(consts, 3)

            def normed(n, i):
                rows = ITEM[i][1]
                pool.wait_ge(raw_copied, KQ * n + (i + 1))
                pool.wait_ge(rinv_made, n * 2 + (i // 2 + 1))
                wait(pool, p_hi_made, KQ * n + (i - 1))
                wait(pool, p_lo_made, KQ * n + (i - 1))
                nc.gpsimd.tensor_tensor(kn[i % 2][0:rows, :].rearrange("p (h d) -> p h d", d=HD),
                                        k_raw[i][0:rows, :].rearrange("p (h d) -> p h d", d=HD),
                                        rinv[0:rows, i, :].unsqueeze(2).broadcast_to([rows, H, HD]), ALU.mult).then_inc(kn_made, 1)

            def layer_scale(t, mv, out, var_made, stat_made, scale_made):
                pool.wait_ge(stat_made, (t + 1) * 2)
                nc.gpsimd.tensor_tensor(out[:, 0:1], mv[:, 1:2], ln_eps[0:N, :], ALU.add).then_inc(var_made, 1)
                pool.wait_ge(var_made, t + 1)
                nc.gpsimd.tensor_tensor(out[:, 1:2], out[:, 0:1], minus_half[0:N, 0:1], ALU.pow).then_inc(scale_made, 1)

            def one(b, par, n, c, m):
                if c is not None:
                    layer_scale(c, mv_h, rstd_hb, var_h, bn_h, rstd_h)
                    pool.wait_ge(x1_made, c + 1)
                    nc.gpsimd.dma_start(xres[:, :], x[bass.ds(c + 1, 1)].rearrange("o t d -> (o t) d")).then_inc(xres_in, 16)
                if n is not None:
                    normed(n, 2)
                    normed(n, 3)
                if m is not None:
                    layer_scale(m, mv_x, rstd_xb, var_x, bn_x, rstd_x)
                    normed(m, 0)
                    normed(m, 1)

            layer_scale(0, mv_x, rstd_xb, var_x, bn_x, rstd_x)
            normed(0, 0)
            normed(0, 1)
            batches(pool, one)
            layer_scale(B - 1, mv_h, rstd_hb, var_h, bn_h, rstd_h)

        @block.scalar
        def _(act):
            def split_w(j):
                act.wait_ge(w_in[j], 16)
                nc.scalar.activation(w_parts[0][:, j, :, :], w_raw[:, j, :, :], ACT.Copy).then_inc(w_hi_made, 1)

            def exps(b, j):
                rows = MT[j % 3][1]
                act.wait_ge(scores_done, b * UNITS + (j + 1))
                wait(act, pv_done, b * UNITS + (j - 1))
                nc.scalar.activation(probs[j % 2][0:rows, :].rearrange("p (a t) -> p a t", a=2),
                                     s_bank[0:rows, :, 0:4 * N], ACT.Exp, scale=float(HD) ** -0.5).then_inc(probs_made, 1)

            def squares(n, i):
                rows = ITEM[i][1]
                act.wait_ge(kq_done, KQ * n + (i + 1))
                wait(act, ss_made, KQ * n + (i - 1))
                nc.scalar.activation(sq[i % 2][0:rows, :], kq_bank[0:rows, i % 2, :], ACT.Square,
                                     scale=float(HD) ** -0.5).then_inc(sq_made, 1)
                wait(act, kn_made, KQ * (n - 1) + (i + 1))
                nc.scalar.activation(k_raw[i][0:rows, :], kq_bank[0:rows, i % 2, :], ACT.Copy).then_inc(raw_copied, 1)

            def rsqrt_guess(n, r):
                act.wait_ge(ms_made, n * 2 + (r + 1))
                nc.scalar.activation(guess[:, :, :], ms[:, :, :].bitcast(mybir.dt.int32), ACT.Exp, scale=GUESS_SCALE,
                                     bias=guess_bias[:, :]).then_inc(guess_made, 1)

            def part_hi(n, i):
                step, rows = ITEM[i]
                act.wait_ge(kn_made, KQ * n + (i + 1))
                wait(act, tr_done, parts_free(n, i))
                src = kn[i % 2][0:rows, :].rearrange("p (h d) -> p h d", d=HD).unsqueeze(2).broadcast_to([rows, H, 2, HD])
                dst = stack4[i % 2][0:rows, :, 0:4:2, :] if step else stack4[i % 2][0:rows, :, 0:2, :]
                nc.scalar.activation(dst, src, ACT.Copy).then_inc(p_hi_made, 1)

            def copy_v(n, mt, par):
                rows = MT[mt][1]
                act.wait_ge(v_done, n * 3 + (mt + 1))
                wait(act, pv_done, (n - 1) * UNITS)
                if isinstance(n, int):
                    act.wait_ge(consts, 8)
                nc.scalar.activation(v_ext[par][0:rows, mt, :, 0:HD], v_bank[0:rows, :].rearrange("p (h d) -> p h d", d=HD),
                                     ACT.Copy).then_inc(v_copied, 1)

            def q_block(n, r, par):
                act.wait_ge(tr_done, n * TR + (8 + r))
                wait(act, scores_done, (n - 1) * UNITS)
                src = tr_bank[:, :].rearrange("p (a t) -> p a t", a=8)
                for h in range(2):
                    last = nc.scalar.activation(q_blk[par][64 * h:64 * h + 64, 8 * r:8 * r + 8, h * N:(h + 1) * N],
                                                src[64 * h:64 * h + 64, :, 0:N], ACT.Copy)
                last.then_inc(tr_used, 1)

            def context_hi(m, r):
                act.wait_ge(ctx_in, (m + 1) * 16)
                wait(act, v_done, (m - 1) * 3 + (2 + r))
                wait(act, kq_done, (m - 1) * KQ + (2 + r))
                cols = slice(CT, M) if r else slice(0, CT)
                nc.scalar.activation(c_parts[0][:, :, cols], c_raw[:, :, cols], ACT.Copy).then_inc(c_hi_made, 1)

            def one(b, par, n, c, m):
                q = 1 - par
                for j in range(UNITS):
                    if b is not None:
                        exps(b, j)
                    if n is not None:
                        if j == 0:
                            part_hi(n, 0)
                            act.wait_ge(xt_made, n + 1)
                            wait(act, kq_done, n * KQ)
                            nc.scalar.activation(x_parts[0][:, :, :], xt[:, :, :], ACT.Copy).then_inc(x_hi_made, 1)
                            squares(n, 2)
                        if j == 1:
                            part_hi(n, 1)
                            copy_v(n, 0, q)
                        if j == 2:
                            squares(n, 3)
                        if j == 3:
                            rsqrt_guess(n, 1)
                        if j == 4:
                            part_hi(n, 2)
                            copy_v(n, 1, q)
                        if j == 5:
                            part_hi(n, 3)
                        if j == 6:
                            copy_v(n, 2, q)
                        if j == 8:
                            q_block(n, 0, q)
                        if j == 9:
                            q_block(n, 1, q)
                    if m is not None:
                        if j == 5:
                            context_hi(m, 0)
                        if j == 7:
                            context_hi(m, 1)
                        if j == 8:
                            squares(m, 0)
                        if j == 10:
                            squares(m, 1)
                        if j == 11:
                            rsqrt_guess(m, 0)
                    if c is not None:
                        tail(c, j)

            def tail(c, j):
                if j == 4:
                    act.wait_ge(ht_made, c + 1)
                    nc.scalar.activation(h_parts[0][:, :, bass.ds(c * N, N)], ht[:, :, :], ACT.Copy).then_inc(h_hi_made, 1)
                if j == 8:
                    act.wait_ge(negm_made, c + 1)
                    nc.scalar.activation(pexp[:, :], lg[:, :], ACT.Exp, bias=neg_m[:, :],
                                         accum_out=pinv[:, 0:1]).then_inc(pexp_made, 1)

            act.wait_ge(consts, 2)
            split_w(0)
            context_hi(0, 0)
            context_hi(0, 1)
            split_w(1)
            squares(0, 0)
            squares(0, 1)
            split_w(2)
            rsqrt_guess(0, 0)
            batches(act, one)

            def split_gu(i, p):
                act.wait_ge(gu_in[p % WR], loads(i, p) * 16)
                nc.scalar.activation(gu_parts[p % WR][0][:, :, :, :].rearrange("p a k f -> p (a k f)"),
                                     raw_gu[p % WR][:, :], ACT.Copy).then_inc(gu_hi_made, 1)

            split_gu(0, 0)
            split_gu(0, 1)
            for j in range(UNITS):
                tail(B - 1, j)
            act.wait_ge(cw_made, B)

            def silu(t, half):
                act.wait_ge(g_done, t * 2 + (half + 1))
                wait(act, gu_mult, t * 2 + (half - 1))
                nc.scalar.activation(act_g[half][:, :], g_bank[:, half, 0:NH], ACT.Silu).then_inc(silu_made, 1)

            def tile(i, p):
                t = i * PER + p
                if p + 2 < PER or not isinstance(i, int) or i < ITER - 1:
                    split_gu(i + (p + 2) // PER, (p + 2) % PER)
                for half in range(2):
                    silu(t, half)
                    act.wait_ge(af_made, t * 2 + (half + 1))
                    nc.scalar.activation(a_parts[HSLOT[p]][0][:, half * NH:(half + 1) * NH], act_f[half][:, :],
                                         ACT.Copy).then_inc(a_hi_made, 1)
                act.wait_ge(dn_in[p % WR], loads(i, p) * 16)
                nc.scalar.activation(dn_parts[HSLOT[p]][0][:, :], raw_dn[p % WR][:, :], ACT.Copy).then_inc(dn_hi_made, 1)

            hidden_tiles(act, tile, lambda i, g: None)

        @block.vector
        def _(dve):
            def split_w(j):
                dve.wait_ge(w_hi_made, j + 1)
                nc.vector.tensor_tensor(w_parts[1][:, j, :, :], w_raw[:, j, :, :], w_parts[0][:, j, :, :].bitcast(F32),
                                        ALU.subtract).then_inc(w_lo_made, 1)

            def sums(n, i):
                rows = ITEM[i][1]
                dve.wait_ge(sq_made, KQ * n + (i + 1))
                if isinstance(n, int):
                    dve.wait_ge(consts, 4)
                nc.vector.tensor_reduce(ss[0:rows, i, :], sq[i % 2][0:rows, :].rearrange("p (h d) -> p h d", d=HD),
                                        AX.X, ALU.add).then_inc(ss_made, 1)

            def variances(n, r):
                dve.wait_ge(ss_made, KQ * n + 2 * (r + 1))
                nc.vector.tensor_scalar(ms[:, :, :], ss[:, 2 * r:2 * r + 2, :], RMS_EPS, None, ALU.add).then_inc(ms_made, 1)

            def rsqrt(n, r):
                dve.wait_ge(guess_made, n * 2 + (r + 1))
                wait(dve, kn_made, KQ * (n - 1) + 2 * (r + 1))
                t = (n * 2 + r) * 5
                y = guess
                for k, out in enumerate((nt[3], rinv)):
                    nc.vector.scalar_tensor_tensor(nt[0][:, :, :], ms[:, :, :], -0.5, y[:, :, :], ALU.mult, ALU.mult).then_inc(newton, 1)
                    dve.wait_ge(newton, t + (3 * k + 1))
                    nc.vector.tensor_tensor(nt[1][:, :, :], nt[0][:, :, :], y[:, :, :], ALU.mult).then_inc(newton, 1)
                    dve.wait_ge(newton, t + (3 * k + 2))
                    last = nc.vector.scalar_tensor_tensor(out[:, :, :] if k == 0 else rinv[:, 2 * r:2 * r + 2, :],
                                                          nt[1][:, :, :], 1.5, y[:, :, :], ALU.add, ALU.mult)
                    if k == 0:
                        last.then_inc(newton, 1)
                        dve.wait_ge(newton, t + 3)
                    y = out
                last.then_inc(rinv_made, 1)

            def part_lo(n, i):
                q, rows = ITEM[i]
                dve.wait_ge(p_hi_made, KQ * n + (i + 1))
                src = kn[i % 2][0:rows, :].rearrange("p (h d) -> p h d", d=HD).unsqueeze(2).broadcast_to([rows, H, 2, HD])
                hi = stack4[i % 2][0:rows, :, 0:4:2, :] if q else stack4[i % 2][0:rows, :, 0:2, :]
                lo = stack4[i % 2][0:rows, :, 1:4:2, :] if q else stack4[i % 2][0:rows, :, 2:4, :]
                nc.vector.tensor_tensor(lo, src, hi, ALU.subtract).then_inc(p_lo_made, 1)

            def k_block(n, mt, r, par, which):
                r0, rows = MT[mt]
                dve.wait_ge(tr_done, n * TR + which)
                wait(dve, scores_done, (n - 1) * UNITS)
                nc.vector.tensor_copy(k_t[par][:, 8 * r:8 * r + 8, r0:r0 + rows],
                                      tr_bank[:, :].rearrange("p (a t) -> p a t", a=8)[:, :, 0:rows]).then_inc(tr_used, 1)

            def o_norm(b, g, par):
                dve.wait_ge(pv_done, b * UNITS + 3 * (g + 1))
                acc = o_bank[0:N, g % 2, 0:GH * HV].rearrange("p (h v) -> p h v", v=HV)
                wait(dve, o_normed, b * HG + (g - 1))
                nc.vector.reciprocal(o_inv[:, g % 2, :].unsqueeze(2), acc[:, :, HD:HV]).then_inc(o_inv_made, 1)
                dve.wait_ge(o_inv_made, b * HG + (g + 1))
                nc.vector.tensor_tensor(x1[par][:, g * GH * HD:(g + 1) * GH * HD].rearrange("p (h d) -> p h d", d=HD),
                                        acc[:, :, 0:HD], o_inv[:, g % 2, :].unsqueeze(2).broadcast_to([N, GH, HD]),
                                        ALU.mult).then_inc(o_normed, 1)

            def layer_stats(t, src, stats, mv, made):
                nc.vector.bn_stats(stats[:, :], src).then_inc(made, 1)
                dve.wait_ge(made, t * 2 + 1)
                carry_wait()
                nc.vector.bn_aggr(mv[:, :], stats[:, :]).then_inc(made, 1)

            def one(b, par, n, c, m):
                q = 1 - par
                for j in range(UNITS):
                    if c is not None and j < 3:
                        tail(c, j, q)
                    if b is not None and j in (4, 7, 10):
                        o_norm(b, j // 3 - 1, par)
                    if c is not None and j == 5:
                        tail(c, j, q)
                    if n is not None:
                        prepare(n, j, q)
                    if c is not None and j >= 3 and j != 5:
                        tail(c, j, q)
                    if n is not None and j == 3:
                        rsqrt(n, 1)
                    if m is not None:
                        if j == 5:
                            context_lo(m, 0)
                        if j == 7:
                            context_lo(m, 1)
                        if j == 8:
                            x_stats(m)
                            sums(m, 0)
                        if j == 10:
                            sums(m, 1)
                            x_normed(m)
                        if j == 11:
                            variances(m, 0)
                            rsqrt(m, 0)

            def prepare(n, j, q):
                if j == 0:
                    dve.wait_ge(tr_done, n * TR + 1)
                    wait(dve, x_hi_made, n)
                    nc.vector.tensor_copy(xt[:, :, :].rearrange("p k t -> p (k t)"),
                                          tr_bank[:, :].bitcast(F32)[:, 0:KT * N]).then_inc(xt_made, 1)
                    part_lo(n, 0)
                if j == 1:
                    dve.wait_ge(x_hi_made, n + 1)
                    nc.vector.tensor_tensor(x_parts[1][:, :, :], xt[:, :, :], x_parts[0][:, :, :].bitcast(F32),
                                            ALU.subtract).then_inc(x_lo_made, 1)
                    k_block(n, 0, 0, q, 2)
                    part_lo(n, 1)
                    sums(n, 2)
                if j == 2:
                    k_block(n, 0, 1, q, 3)
                    sums(n, 3)
                    variances(n, 1)
                if j == 3:
                    k_block(n, 1, 0, q, 4)
                if j == 4:
                    k_block(n, 1, 1, q, 5)
                    part_lo(n, 2)
                if j == 5:
                    part_lo(n, 3)
                if j == 6:
                    k_block(n, 2, 0, q, 6)
                if j == 7:
                    k_block(n, 2, 1, q, 7)

            def context_lo(m, r):
                dve.wait_ge(c_hi_made, m * 2 + (1 + r))
                cols = slice(CT, M) if r else slice(0, CT)
                nc.vector.tensor_tensor(c_parts[1][:, :, cols], c_raw[:, :, cols], c_parts[0][:, :, cols].bitcast(F32),
                                        ALU.subtract).then_inc(c_lo_made, 1)

            def x_stats(m):
                dve.wait_ge(x_in, (m + 1) * 16)
                layer_stats(m, xin[:, :], stats_x, mv_x, bn_x)

            def x_normed(m):
                dve.wait_ge(rstd_x, m + 1)
                nc.vector.tensor_scalar(xn[:, :], xin[:, :], mv_x[:, 0:1], rstd_xb[:, 1:2],
                                        ALU.subtract, ALU.mult).then_inc(xn_made, 1)

            def tail(c, j, par):
                if j == 0:
                    o_norm(c, 3, par)
                    dve.wait_ge(xres_in, (c + 1) * 16)
                    dve.wait_ge(o_normed, (c + 1) * HG)
                    nc.vector.tensor_tensor(x1[par][:, :], x1[par][:, :], xres[:, :], ALU.add).then_inc(x1_made, 1)
                    dve.wait_ge(x1_made, c + 1)
                    layer_stats(c, x1[par][:, :], stats_h, mv_h, bn_h)
                if j == 1:
                    dve.wait_ge(rstd_h, c + 1)
                    nc.vector.tensor_scalar(hn[:, :], x1[par][:, :], mv_h[:, 0:1], rstd_hb[:, 1:2],
                                            ALU.subtract, ALU.mult).then_inc(hn_made, 1)
                if j == 3:
                    dve.wait_ge(ht_done, c + 1)
                    nc.vector.tensor_copy(ht[:, :, :].rearrange("p k t -> p (k t)"), v_bank[:, 0:KT * N]).then_inc(ht_made, 1)
                if j == 4:
                    dve.wait_ge(h_hi_made, c + 1)
                    nc.vector.tensor_tensor(h_parts[1][:, :, bass.ds(c * N, N)], ht[:, :, :],
                                            h_parts[0][:, :, bass.ds(c * N, N)].bitcast(F32), ALU.subtract).then_inc(h_lo_made, 1)
                if j == 5:
                    dve.wait_ge(x1t_done, c + 1)
                    nc.vector.tensor_copy(y_sum[:, :, bass.ds(c * N, N)],
                                          v_bank[:, 0:KT * N].rearrange("p (k t) -> p k t", k=KT)).then_inc(x1t_made, 1)
                if j == 7:
                    dve.wait_ge(lg_done, c + 1)
                    nc.vector.tensor_copy(lg[:, :], v_bank[0:N, 0:E]).then_inc(lg_made, 1)
                    dve.wait_ge(lg_made, c + 1)
                    carry_wait()
                    nc.vector.max(top_l[:, :], lg[:, :]).then_inc(gate_step, 1)
                    dve.wait_ge(gate_step, c * 5 + 1)
                    nc.vector.tensor_scalar(neg_m[:, :], top_l[:, 0:1], -1.0, None, ALU.mult).then_inc(negm_made, 1)
                if j == 8:
                    dve.wait_ge(pexp_made, c + 1)
                    nc.vector.reciprocal(pinv[:, 1:2], pinv[:, 0:1]).then_inc(gate_step, 1)
                    dve.wait_ge(gate_step, c * 5 + 2)
                    nc.vector.tensor_scalar(sc_ext[:, 0:E], pexp[:, :], pinv[:, 1:2], None, ALU.mult).then_inc(gate_step, 1)
                    dve.wait_ge(gate_step, c * 5 + 3)
                    dve.wait_ge(consts, 12)
                    carry_wait()
                    nc.vector.max(top_l[:, :], sc_ext[:, 0:E]).then_inc(gate_step, 1)
                    dve.wait_ge(gate_step, c * 5 + 4)
                    nc.vector.tensor_copy(top_s[:, 0:TOP_K], top_l[:, 0:TOP_K]).then_inc(gate_step, 1)
                    dve.wait_ge(gate_step, c * 5 + 5)
                    carry_wait()
                    nc.vector.match_replace(rest[:, :], top_s[:, :], sc_ext[:, :], 0.0).then_inc(rest_made, 1)
                    dve.wait_ge(rest_made, c + 1)
                    nc.vector.tensor_tensor(cw[:, :], sc_ext[:, 0:E], rest[:, 0:E], ALU.subtract).then_inc(cw_made, 1)
                if j == 11:
                    dve.wait_ge(cwt_done, c + 1)
                    nc.vector.tensor_copy(cw_t[:, bass.ds(c * N, N)], v_bank[0:E, 0:N]).then_inc(cwt_made, 1)

            split_w(0)
            context_lo(0, 0)
            context_lo(0, 1)
            split_w(1)
            x_stats(0)
            x_normed(0)
            sums(0, 0)
            sums(0, 1)
            variances(0, 0)
            rsqrt(0, 0)
            split_w(2)
            dve.wait_ge(eye_in, 16)
            nc.vector.tensor_copy(id16[:, :], id32[:, :]).then_inc(id16_made, 1)
            batches(dve, one)

            def split_gu(i, p):
                dve.wait_ge(gu_hi_made, i * PER + (p + 1))
                nc.vector.tensor_tensor(gu_parts[p % WR][1][:, :, :, :].rearrange("p a k f -> p (a k f)"), raw_gu[p % WR][:, :],
                                        gu_parts[p % WR][0][:, :, :, :].rearrange("p a k f -> p (a k f)").bitcast(F32),
                                        ALU.subtract).then_inc(gu_lo_made, 1)

            split_gu(0, 0)
            split_gu(0, 1)
            for j in range(UNITS):
                tail(B - 1, j, 1)

            def tile(i, p):
                t = i * PER + p
                if p + 2 < PER or not isinstance(i, int) or i < ITER - 1:
                    split_gu(i + (p + 2) // PER, (p + 2) % PER)
                for half in range(2):
                    k = t * 2 + (half + 1)
                    cols = slice(half * NH, (half + 1) * NH)
                    dve.wait_ge(silu_made, k)
                    dve.wait_ge(u_done, k)
                    nc.vector.tensor_tensor(act_u[half][:, :], act_g[half][:, :], u_bank[:, half, 0:NH], ALU.mult).then_inc(gu_mult, 1)
                    dve.wait_ge(gu_mult, k)
                    wait(dve, a_hi_made, k - 2)
                    segments = cw_segments(p)
                    for n, (r0, r1, e) in enumerate(segments):
                        dve.wait_ge(cwb_in[e], (i + 1) * 16)
                        last = nc.vector.tensor_tensor(act_f[half][r0:r1, :], act_u[half][r0:r1, :], cw_b[e][r0:r1, cols], ALU.mult)
                    last.then_inc(af_made, 1)
                    dve.wait_ge(a_hi_made, k)
                    a = a_parts[HSLOT[p]]
                    nc.vector.tensor_tensor(a[1][:, cols], act_f[half][:, :], a[0][:, cols].bitcast(F32),
                                            ALU.subtract).then_inc(a_lo_made, 1)
                dve.wait_ge(dn_hi_made, t + 1)
                d = dn_parts[HSLOT[p]]
                nc.vector.tensor_tensor(d[1][:, :], raw_dn[p % WR][:, :], d[0][:, :].bitcast(F32),
                                        ALU.subtract).then_inc(dn_lo_made, 1)

            def add_group(i, g):
                for idx in range(2 * KT):
                    dt, half = idx // 2, idx % 2
                    k = i * (6 * KT) + (2 * KT * g + idx + 1)
                    dve.wait_ge(y_done, k)
                    y = y_sum[:, dt, half * NH:(half + 1) * NH]
                    nc.vector.tensor_tensor(y, y, y_bank[:, idx % 4, 0:NH], ALU.add).then_inc(y_added, 1)

            hidden_tiles(dve, tile, add_group)

        @block.tensor
        def _(pe):
            def project(out, rows, lhs, w, col):
                for k in range(KT):
                    for s, (a, b) in enumerate(CASES):
                        last = nc.tensor.matmul(out, lhs[a][:, k, col:col + rows], w_parts[b][:, w, k, :],
                                                start=(k == 0 and s == 0), stop=(k == KT - 1 and s == 2))
                return last

            def project_k(n, mt, i):
                if mt == 0 or mt == 2:
                    pe.wait_ge(c_hi_made, n * 2 + (1 if mt == 0 else 2))
                    pe.wait_ge(c_lo_made, n * 2 + (1 if mt == 0 else 2))
                    pe.wait_ge(w_lo_made, 1)
                wait(pe, raw_copied, KQ * n + (i - 1))
                project(kq_bank[0:MT[mt][1], i % 2, :], MT[mt][1], c_parts, 0, MT[mt][0]).then_inc(kq_done, 1)

            def project_q(n):
                pe.wait_ge(x_hi_made, n + 1)
                pe.wait_ge(x_lo_made, n + 1)
                pe.wait_ge(w_lo_made, 3)
                wait(pe, raw_copied, KQ * n + 2)
                project(kq_bank[0:N, 1, :], N, x_parts, 2, 0).then_inc(kq_done, 1)

            def project_v(n, mt):
                pe.wait_ge(w_lo_made, 2)
                project(v_bank[0:MT[mt][1], :], MT[mt][1], c_parts, 1, MT[mt][0]).then_inc(v_done, 1)

            def bank_free(n, which):
                if which == 1:
                    pe.wait_ge(xt_made, n + 1)
                else:
                    wait(pe, tr_used, n * (TR - 1) + max(which - 1, 0))

            def stack_transposes(n, i, r, which):
                rows = ITEM[i][1]
                pe.wait_ge(id16_made, 1)
                pe.wait_ge(p_lo_made, KQ * n + (i + 1))
                bank_free(n, which)
                for a in range(8):
                    pair = stack4[i % 2][0:rows, 2 * (8 * r + a):2 * (8 * r + a) + 2, :, :].rearrange("p h s d -> p (h s d)")
                    last = nc.tensor.transpose(tr_bank[:, a * P:a * P + rows], pair, id16[0:rows, 0:rows])
                last.then_inc(tr_done, 1)

            def scores(b, j, par):
                g, mt = j // 3, j % 3
                r0, rows = MT[mt]
                wait(pe, probs_made, b * UNITS + j)
                if j == 0:
                    pe.wait_ge(tr_used, (b + 1) * (TR - 1))
                    pe.wait_ge(xt_made, b + 1)
                for a in range(4):
                    last = nc.tensor.matmul(s_bank[0:rows, a // 2, (a % 2) * 2 * N:(a % 2 + 1) * 2 * N],
                                            k_t[par][:, 4 * g + a, r0:r0 + rows], q_blk[par][:, 4 * g + a, :],
                                            start=True, stop=True)
                last.then_inc(scores_done, 1)

            def values(b, j, par):
                g, mt = j // 3, j % 3
                rows = MT[mt][1]
                pe.wait_ge(probs_made, b * UNITS + (j + 1))
                if j == 0:
                    pe.wait_ge(v_copied, (b + 1) * 3)
                if mt == 0:
                    wait(pe, o_normed, b * HG + (g - 1))
                for h in range(GH):
                    last = nc.tensor.matmul(o_bank[0:N, g % 2, h * HV:(h + 1) * HV], probs[j % 2][0:rows, h * N:(h + 1) * N],
                                            v_ext[par][0:rows, mt, g * GH + h, :], start=(mt == 0 and h == 0), stop=(mt == 2),
                                            skip_group_check=True)
                last.then_inc(pv_done, 1)

            def one(b, par, n, c, m):
                q = 1 - par
                for j in range(UNITS):
                    if b is not None:
                        scores(b, j, par)
                    if c is not None and j == 0:
                        values(c, UNITS - 1, q)
                    if n is not None:
                        if j == 0:
                            pe.wait_ge(xn_made, n + 1)
                            pe.wait_ge(eye_in, 16)
                            bank_free(n, 0)
                            for k in range(KT):
                                last = nc.tensor.transpose(tr_bank[:, :].bitcast(F32)[:, k * N:(k + 1) * N],
                                                           xn[:, k * P:(k + 1) * P], id32[0:N, 0:N])
                            last.then_inc(tr_done, 1)
                            project_k(n, 2, 2)
                        if j == 1:
                            wait(pe, v_copied, n * 3)
                            if c is not None:
                                pe.wait_ge(x1_made, c + 1)
                            project_v(n, 0)
                            stack_transposes(n, 0, 0, 1)
                        if j == 2:
                            project_q(n)
                            stack_transposes(n, 0, 1, 2)
                        if j == 3:
                            stack_transposes(n, 1, 0, 3)
                            pe.wait_ge(v_copied, n * 3 + 1)
                        if j == 4:
                            if c is not None:
                                pe.wait_ge(ht_made, c + 1)
                            project_v(n, 1)
                            stack_transposes(n, 1, 1, 4)
                        if j == 5:
                            pe.wait_ge(v_copied, n * 3 + 2)
                        if j == 6:
                            stack_transposes(n, 2, 0, 5)
                            if c is not None:
                                pe.wait_ge(x1t_made, c + 1)
                            project_v(n, 2)
                        if j == 7:
                            stack_transposes(n, 2, 1, 6)
                            pe.wait_ge(v_copied, n * 3 + 3)
                        if j == 8:
                            stack_transposes(n, 3, 0, 7)
                        if j == 9:
                            stack_transposes(n, 3, 1, 8)
                    if m is not None:
                        if j == 8:
                            project_k(m, 0, 0)
                        if j == 10:
                            project_k(m, 1, 1)
                    if c is not None:
                        tail(c, j, q)
                    if b is not None and j > 0:
                        values(b, j - 1, par)

            def tail(c, j, par):
                if j == 3:
                    pe.wait_ge(hn_made, c + 1)
                    for k in range(KT):
                        last = nc.tensor.transpose(v_bank[:, k * N:(k + 1) * N], hn[:, k * P:(k + 1) * P], id32[0:N, 0:N])
                    last.then_inc(ht_done, 1)
                if j == 5:
                    pe.wait_ge(ht_made, c + 1)
                    for k in range(KT):
                        last = nc.tensor.transpose(v_bank[:, k * N:(k + 1) * N], x1[par][:, k * P:(k + 1) * P], id32[0:N, 0:N])
                    last.then_inc(x1t_done, 1)
                if j == 7:
                    pe.wait_ge(x1t_made, c + 1)
                    pe.wait_ge(gate_in, 16)
                    for k in range(KT):
                        last = nc.tensor.matmul(v_bank[0:N, 0:E], ht[:, k, :], gate_w[:, k, :], start=(k == 0), stop=(k == KT - 1))
                    last.then_inc(lg_done, 1)
                if j == 11:
                    pe.wait_ge(lg_made, c + 1)
                    pe.wait_ge(cw_made, c + 1)
                    nc.tensor.transpose(v_bank[0:E, 0:N], cw[:, :], id32[0:N, 0:N]).then_inc(cwt_done, 1)

            project_k(0, 0, 0)
            project_k(0, 1, 1)
            batches(pe, one)
            values(B - 1, UNITS - 1, 1)
            for j in range(UNITS - 1):
                tail(B - 1, j, 1)
            pe.wait_ge(h_hi_made, B)
            pe.wait_ge(h_lo_made, B)

            def gate_up(i, p, half):
                t = i * PER + p
                pe.wait_ge(gu_lo_made, t + 1)
                w = gu_parts[p % WR]
                for s, (bank, freed, done) in enumerate(((g_bank, silu_made, g_done), (u_bank, gu_mult, u_done))):
                    wait(pe, freed, t * 2 + (half - 1))
                    for k in range(KT):
                        for m, (a, b) in enumerate(CASES):
                            last = nc.tensor.matmul(bank[:, half, 0:NH], w[a][:, s, k, :], h_parts[b][:, k, half * NH:(half + 1) * NH],
                                                    start=(k == 0 and m == 0), stop=(k == KT - 1 and m == 2))
                    last.then_inc(done, 1)

            def tile(i, p):
                gate_up(i, p, 0)
                if isinstance(i, int) and i == 0 and p == 0:
                    tail(B - 1, UNITS - 1, 1)
                gate_up(i, p, 1)

            def down(i, g):
                first, end = GROUPS[g]
                t_end = i * PER + end
                pe.wait_ge(a_lo_made, t_end * 2)
                pe.wait_ge(dn_lo_made, t_end)
                for idx in range(2 * KT):
                    dt, half = idx // 2, idx % 2
                    if idx >= 4:
                        pe.wait_ge(y_added, i * (6 * KT) + (2 * KT * g + idx - 3))
                    for p in range(first, end):
                        for m, (a, b) in enumerate(CASES):
                            last = nc.tensor.matmul(y_bank[:, idx % 4, 0:NH], dn_parts[HSLOT[p]][a][:, dt * P:(dt + 1) * P],
                                                    a_parts[HSLOT[p]][b][:, half * NH:(half + 1) * NH],
                                                    start=(p == first and m == 0), stop=(p == end - 1 and m == 2))
                    last.then_inc(y_done, 1)

            hidden_tiles(pe, tile, down)


def kernel(x, ctx_2048, L0_xattn_Wq, L0_xattn_Wk, L0_xattn_Wv, L0_ffn_gate_w, L0_ffn_w_gate, L0_ffn_w_up, L0_ffn_w_down):
    import concourse.bacc as bacc
    import numpy as np
    from concourse.bass_utils import run_bass_kernel_spmd

    B, N, D = x.shape
    M = ctx_2048.shape[1]
    E, F, _ = L0_ffn_w_gate.shape
    KT, TILES = D // P, E * F // P

    def k_major(w):
        return np.asarray(w).T.reshape(KT, P, -1).transpose(1, 0, 2)

    kv = np.concatenate([np.asarray(L0_xattn_Wk), np.asarray(L0_xattn_Wv)], axis=0)
    w_kvq = np.stack([k_major(kv[0::2]), k_major(kv[1::2]), k_major(L0_xattn_Wq)], axis=1)
    ctx_t = np.asarray(ctx_2048).transpose(0, 2, 1).reshape(B, KT, P, M).transpose(0, 2, 1, 3)

    def hidden_major(w):
        return np.asarray(w).reshape(TILES, P, KT, P).transpose(0, 3, 2, 1).reshape(TILES, P, KT * P)

    down = np.asarray(L0_ffn_w_down).transpose(0, 2, 1).reshape(TILES, P, D)
    w_moe = np.concatenate([hidden_major(L0_ffn_w_gate), hidden_major(L0_ffn_w_up), down], axis=2)

    ins = {
        "x": np.asarray(x), "ctx_t": ctx_t, "w_kvq": w_kvq, "gate_t": k_major(L0_ffn_gate_w), "w_moe": w_moe,
        "eye": np.eye(P, dtype=np.float32),
    }
    ins = {f"in_{name}": np.ascontiguousarray(a) for name, a in ins.items()}
    nc = bacc.Bacc("TRN2", target_bir_lowering=False, num_devices=1)
    aps = [nc.dram_tensor(name, a.shape, mybir.dt.from_np(a.dtype), kind="ExternalInput").ap() for name, a in ins.items()]
    out = nc.dram_tensor("out_t", (KT, P, B * N), F32, kind="ExternalOutput").ap()
    xattn_moe_program(nc, *aps, out)
    r = run_bass_kernel_spmd(nc, [ins], core_ids=[0])
    return r.results[0]["out_t"].reshape(D, B * N).T.reshape(B, N, D)
```

```python
import math
from contextlib import ExitStack

import concourse.bass as bass
from concourse import mybir

F32 = mybir.dt.float32
F32R = mybir.dt.float32r
F16 = mybir.dt.float16
ALU = mybir.AluOpType
ACT = mybir.ActivationFunctionType
AX = mybir.AxisListType

P = 128
LN_EPS = 1e-5
RMS_EPS = 1e-6
TOP_K = 6
UNIT = 64.0
GUESS_SCALE = -0.5 * math.log(2.0) / 2 ** 23
GUESS_BIAS = 0.5 * math.log(2.0) * (127 - 0.043)


def xattn_moe_program(nc, x, ctx_t, w_kvq, gate_t, w_moe, eye, out_t):
    B, N, D = x.shape
    _, _, KT, M = ctx_t.shape
    E = gate_t.shape[2]
    TILES = w_moe.shape[0]
    FE = TILES * P // E
    H = 32
    HD = D // H
    HV = HD + 1
    T = B * N
    NH = T // 2
    CT = 2 * P
    MT = [(0, P), (P, P), (2 * P, M - 2 * P)]
    PAIRS = H // 2
    HG = 4
    GH = H // HG
    UNITS = HG * len(MT)
    KQ = 4
    TR = 9
    PER = 11
    EPER = PER * P // FE
    ITER = TILES // PER
    assert PER * P == EPER * FE and ITER * PER == TILES and D == KT * P and T == 2 * NH
    GROUPS = [(0, 4), (4, 8), (8, 11)]
    HSLOT = [0, 1, 2, 3, 4, 5, 6, 7, 1, 2, 3]
    WR = 4
    CASES = [(0, 0), (0, 1), (1, 0)]

    scratch = nc.dram_tensor("combine_scratch", (E, T), F32, kind="Internal").ap()

    with ExitStack() as ctx:
        def sem(name):
            return ctx.enter_context(nc.semaphore(name))

        def tensors(stack):
            return (lambda name, shape, dt=F32: stack.enter_context(nc.sbuf_tensor(name, shape, dt)),
                    lambda name, shape, dt=F32: stack.enter_context(nc.psum_tensor(name, shape, dt)))

        staging = ExitStack()
        sb, _ = tensors(staging)
        w_raw = sb("w_raw", [P, 3, KT, D])
        staging.close()

        sb, _ = tensors(ctx)
        y_sum = sb("y_sum", [P, KT, T])
        h_parts = [sb("h_hi", [P, KT, T], F32R), sb("h_lo", [P, KT, T], F32R)]
        id32 = sb("id32", [P, P])
        id16 = sb("id16", [P, P], F16)
        gate_w = sb("gate_w", [P, KT, E])
        cw = sb("cw", [N, E])
        cw_t = sb("cw_t", [E, T])
        minus_half = sb("minus_half", [P, 1])
        guess_bias = sb("guess_bias", [P, 1])
        ln_eps = sb("ln_eps", [P, 1])
        carrier = sb("carrier", [1, 1])

        att = ExitStack()
        sb, ps = tensors(att)
        w_parts = [sb("w_hi", [P, 3, KT, D], F32R), sb("w_lo", [P, 3, KT, D], F32R)]
        c_raw = sb("c_raw", [P, KT, M])
        c_parts = [sb("c_hi", [P, KT, M], F32R), sb("c_lo", [P, KT, M], F32R)]
        xin = sb("xin", [N, D])
        xres = sb("xres", [N, D])
        xn = sb("xn", [N, D])
        xt = sb("xt", [P, KT, N])
        x_parts = [sb("xt_hi", [P, KT, N], F32R), sb("xt_lo", [P, KT, N], F32R)]
        stats_x, mv_x, rstd_xb = sb("stats_x", [N, 6]), sb("mv_x", [N, 2]), sb("rstd_xb", [N, 2])
        stats_h, mv_h, rstd_hb = sb("stats_h", [N, 6]), sb("mv_h", [N, 2]), sb("rstd_hb", [N, 2])
        k_raw = [sb(f"k_raw{i}", [P, D]) for i in range(KQ)]
        sq = [sb(f"sq{i}", [P, D]) for i in range(2)]
        ss = sb("ss", [P, KQ, H])
        ms, guess = sb("ms", [P, 2, H]), sb("guess", [P, 2, H])
        nt = [sb(f"nt{i}", [P, 2, H]) for i in range(3)]
        rinv = sb("rinv", [P, KQ, H])
        kn = [sb(f"kn{i}", [P, D]) for i in range(2)]
        stack4 = [sb(f"stack4_{i}", [P, H, 4, HD], F16) for i in range(2)]
        k_t = [sb(f"k_t{i}", [P, PAIRS, M], F16) for i in range(2)]
        q_blk = [sb(f"q_blk{i}", [P, PAIRS, 2 * N], F16) for i in range(2)]
        v_ext = [sb(f"v_ext{i}", [P, 3, H, HV]) for i in range(2)]
        probs = [sb(f"probs{i}", [P, GH * N]) for i in range(2)]
        o_inv = sb("o_inv", [N, 2, GH])
        x1 = [sb(f"x1_{i}", [N, D]) for i in range(2)]
        hn = sb("hn", [N, D])
        ht = sb("ht", [P, KT, N])
        lg = sb("lg", [N, E])
        top_l = sb("top_l", [N, 8])
        neg_m = sb("neg_m", [N, 1])
        pexp = sb("pexp", [N, E])
        pinv = sb("pinv", [N, 2])
        sc_ext = sb("sc_ext", [N, E + 2])
        top_s = sb("top_s", [N, 8])
        rest = sb("rest", [N, E + 2])
        s_bank = ps("s_bank", [P, 2, 512])
        kq_bank = ps("kq_bank", [P, 2, 512])
        o_bank = ps("o_bank", [P, 2, 512])
        tr_bank = ps("tr_bank", [P, 1024], F16)
        v_bank = ps("v_bank", [P, 512])
        att.close()

        sb, ps = tensors(ctx)
        raw_gu = [sb(f"raw_gu{i}", [P, 2 * D]) for i in range(WR)]
        raw_dn = [sb(f"raw_dn{i}", [P, D]) for i in range(WR)]
        gu_parts = [[sb(f"gu_hi{i}", [P, 2, KT, P], F32R), sb(f"gu_lo{i}", [P, 2, KT, P], F32R)] for i in range(WR)]
        dn_parts = [[sb(f"dn_hi{i}", [P, D], F32R), sb(f"dn_lo{i}", [P, D], F32R)] for i in range(8)]
        a_parts = [[sb(f"a_hi{i}", [P, T], F32R), sb(f"a_lo{i}", [P, T], F32R)] for i in range(8)]
        cw_b = [sb(f"cw_b{i}", [P, T]) for i in range(EPER)]
        act_g = [sb(f"act_g{i}", [P, NH]) for i in range(2)]
        act_u = [sb(f"act_u{i}", [P, NH]) for i in range(2)]
        act_f = [sb(f"act_f{i}", [P, NH]) for i in range(2)]
        g_bank = ps("g_bank", [P, 2, 512])
        u_bank = ps("u_bank", [P, 2, 512])
        y_bank = ps("y_bank", [P, 4, 512])

        eye_in, gate_in = sem("eye_in"), sem("gate_in")
        w_in = [sem(f"w_in{i}") for i in range(3)]
        ctx_in, x_in, xres_in = sem("ctx_in"), sem("x_in"), sem("xres_in")
        consts = sem("consts")
        id16_made, table_loaded = sem("id16_made"), sem("table_loaded")
        w_hi_made, w_lo_made = sem("w_hi_made"), [sem(f"w_lo_made{i}") for i in range(3)]
        c_hi_made, c_lo_made = sem("c_hi_made"), sem("c_lo_made")
        bn_x, var_x, rstd_x, xn_made = sem("bn_x"), sem("var_x"), sem("rstd_x"), sem("xn_made")
        xt_made, x_hi_made, x_lo_made = sem("xt_made"), sem("x_hi_made"), sem("x_lo_made")
        kq_done, v_done = sem("kq_done"), sem("v_done")
        sq_made, ss_made, raw_copied = sem("sq_made"), sem("ss_made"), sem("raw_copied")
        ms_made, guess_made, newton, rinv_made = sem("ms_made"), sem("guess_made"), sem("newton"), sem("rinv_made")
        kn_made, p_hi_made, p_lo_made = sem("kn_made"), sem("p_hi_made"), sem("p_lo_made")
        v_copied = sem("v_copied")
        tr_done, tr_used = sem("tr_done"), sem("tr_used")
        scores_done, probs_made, pv_done, o_normed = sem("scores_done"), sem("probs_made"), sem("pv_done"), sem("o_normed")
        o_inv_made, x1_made = sem("o_inv_made"), sem("x1_made")
        bn_h, var_h, rstd_h, hn_made = sem("bn_h"), sem("var_h"), sem("rstd_h"), sem("hn_made")
        ht_done, ht_made, h_hi_made, h_lo_made = sem("ht_done"), sem("ht_made"), sem("h_hi_made"), sem("h_lo_made")
        x1t_done, x1t_made = sem("x1t_done"), sem("x1t_made")
        lg_done, lg_made, negm_made, pexp_made = sem("lg_done"), sem("lg_made"), sem("negm_made"), sem("pexp_made")
        gate_step, cw_made, cwt_done, cwt_made = sem("gate_step"), sem("cw_made"), sem("cwt_done"), sem("cwt_made")
        rest_made = sem("rest_made")
        scratch_written = sem("scratch_written")
        gu_in = [sem(f"gu_in{i}") for i in range(WR)]
        dn_in = [sem(f"dn_in{i}") for i in range(WR)]
        cwb_in = [sem(f"cwb_in{i}") for i in range(EPER)]
        gu_hi_made, gu_lo_made, dn_hi_made, dn_lo_made = sem("gu_hi_made"), sem("gu_lo_made"), sem("dn_hi_made"), sem("dn_lo_made")
        g_done, u_done = sem("g_done"), sem("u_done")
        silu_made, gu_mult, af_made, a_hi_made, a_lo_made = sem("silu_made"), sem("gu_mult"), sem("af_made"), sem("a_hi_made"), sem("a_lo_made")
        y_done, y_added, out_written = sem("y_done"), sem("y_added"), sem("out_written")

        block = ctx.enter_context(nc.Block())

        def wait(eng, semaphore, value):
            if not isinstance(value, int) or value > 0:
                eng.wait_ge(semaphore, value)

        def carry_wait():
            nc.vector.memset(carrier[:, :], 0.0)

        def is_first(n):
            return isinstance(n, int) and n == 0

        def batches(eng, one):
            one(None, 1, 0, None, 1)
            one(0, 0, 1, None, 2)
            with eng.Fori(0, (B - 4) // 2) as i:
                one(i * 2 + 1, 1, i * 2 + 2, i * 2, i * 2 + 3)
                one(i * 2 + 2, 0, i * 2 + 3, i * 2 + 1, i * 2 + 4)
            one(B - 3, 1, B - 2, B - 4, B - 1)
            one(B - 2, 0, B - 1, B - 3, None)
            one(B - 1, 1, None, B - 2, None)

        def hidden_tiles(eng, one, group):
            def round_(i, more):
                for p in range(1, PER):
                    one(i, p)
                    if p == 4:
                        group(i, 0)
                    if p == 8:
                        group(i, 1)
                if more:
                    one(i + 1, 0)
                group(i, 2)
            one(0, 0)
            with eng.Fori(0, ITER - 1) as i:
                round_(i, True)
            round_(ITER - 1, False)

        ITEM = [(0, MT[0][1]), (0, MT[1][1]), (0, MT[2][1]), (1, N)]
        LAST_TR = [3, 5, 7, 9]

        def parts_free(n, item):
            return TR * n + LAST_TR[item - 2] - (TR if item < 2 else 0)

        def slot_user(p):
            return p - WR if p >= WR else max(q for q in range(PER) if q % WR == p % WR) - PER

        def loads(i, p):
            return i * len([q for q in range(PER) if q % WR == p % WR]) + p // WR + 1

        def cw_segments(p):
            cuts = {0, P} | {e * FE - p * P for e in range(EPER) if 0 < e * FE - p * P < P}
            if 32 in cuts:
                cuts.add(64)
            cuts = sorted(cuts)
            return [(a, b, (p * P + a) // FE) for a, b in zip(cuts, cuts[1:])]

        @block.sync
        def _(sp):
            sp.dma_start(w_raw[:, 0, :, :], w_kvq[:, 0, :, :]).then_inc(w_in[0], 16)
            sp.dma_start(c_raw[:, :, :], ctx_t[0]).then_inc(ctx_in, 16)
            sp.dma_start(xin[:, :], x[0]).then_inc(x_in, 16)
            sp.dma_start(id32[:, :], eye).then_inc(eye_in, 16)
            for j in range(1, 3):
                sp.dma_start(w_raw[:, j, :, :], w_kvq[:, j, :, :]).then_inc(w_in[j], 16)
            sp.dma_start(gate_w[:, :, :], gate_t).then_inc(gate_in, 16)
            with sp.Fori(1, B) as n:
                sp.wait_ge(c_hi_made, n * 2)
                sp.wait_ge(c_lo_made, n * 2)
                sp.dma_start(c_raw[:, :, :], ctx_t[bass.ds(n, 1)].rearrange("o p k m -> (o p) k m")).then_inc(ctx_in, 16)
                sp.wait_ge(xn_made, n)
                sp.dma_start(xin[:, :], x[bass.ds(n, 1)].rearrange("o t d -> (o t) d")).then_inc(x_in, 16)
            sp.wait_ge(kq_done, KQ * B)
            sp.wait_ge(v_done, 3 * B)
            for t in range(WR):
                sp.dma_start(raw_gu[t][:, :], w_moe[t, :, 0:2 * D]).then_inc(gu_in[t], 16)
            for t in range(WR):
                sp.dma_start(raw_dn[t][:, :], w_moe[t, :, 2 * D:3 * D]).then_inc(dn_in[t], 16)
            sp.wait_ge(cwt_made, B + 1)
            sp.dma_start(scratch, cw_t[:, :]).then_inc(scratch_written, 16)
            sp.wait_ge(scratch_written, 16)
            for e in range(EPER):
                sp.dma_start(cw_b[e][:, :], scratch[e].partition_broadcast(P)).then_inc(cwb_in[e], 16)

            def load(i, q, ahead, ring, cols, sems, hi_made, lo_made):
                p = (q + ahead) % PER
                user = slot_user(p) + PER * (i + (q + ahead) // PER)
                sp.wait_ge(hi_made, user + 1)
                sp.wait_ge(lo_made, user + 1)
                sp.dma_start(ring[p % WR][:, :], w_moe[bass.ds(i * PER + (q + ahead), 1), :, cols].rearrange("o p n -> (o p) n"))\
                  .then_inc(sems[p % WR], 16)

            def load_round(i, last):
                for q in range(PER):
                    if not last or q + WR < PER:
                        load(i, q, WR, raw_gu, slice(0, 2 * D), gu_in, gu_hi_made, gu_lo_made)
                    if not last or q + WR < PER:
                        load(i, q, WR, raw_dn, slice(2 * D, 3 * D), dn_in, dn_hi_made, dn_lo_made)
                    for e in range(EPER):
                        last_tile = ((e + 1) * FE - 1) // P
                        if q == min(last_tile + 1, PER - 1) and not last:
                            sp.wait_ge(af_made, (i * PER + last_tile + 1) * 2)
                            sp.dma_start(cw_b[e][:, :], scratch[bass.ds(i * EPER + (EPER + e), 1)]
                                         .rearrange("o t -> (o t)").partition_broadcast(P)).then_inc(cwb_in[e], 16)

            with sp.Fori(0, ITER - 1) as i:
                load_round(i, False)
            load_round(ITER - 1, True)
            for idx in range(2 * KT):
                dt, half = idx // 2, idx % 2
                sp.wait_ge(y_added, 3 * 2 * KT * ITER - 2 * KT + idx + 1)
                sp.dma_start(out_t[dt, :, half * NH:(half + 1) * NH], y_sum[:, dt, half * NH:(half + 1) * NH])\
                  .then_inc(out_written, 16)
            sp.wait_ge(out_written, 16 * 2 * KT)

        @block.gpsimd
        def _(pool):
            pool.dma_start(xres[:, :], x[0]).then_inc(xres_in, 16)
            nc.gpsimd.memset(minus_half[:, :], -0.5).then_inc(consts, 1)
            nc.gpsimd.memset(guess_bias[:, :], GUESS_BIAS).then_inc(consts, 1)
            nc.gpsimd.memset(ln_eps[:, :], LN_EPS).then_inc(consts, 1)
            nc.gpsimd.memset(ss[:, :, :], 1.0).then_inc(consts, 1)
            for i in range(2):
                nc.gpsimd.memset(q_blk[i][:, :, :], 0.0).then_inc(consts, 1)
                nc.gpsimd.memset(v_ext[i][:, :, :, :], 1.0).then_inc(consts, 1)
            nc.gpsimd.memset(sc_ext[:, E:E + 1], -1.0).then_inc(consts, 1)
            nc.gpsimd.memset(sc_ext[:, E + 1:E + 2], -2.0).then_inc(consts, 1)
            nc.gpsimd.memset(top_s[:, TOP_K:TOP_K + 1], -1.0).then_inc(consts, 1)
            nc.gpsimd.memset(top_s[:, TOP_K + 1:8], -2.0).then_inc(consts, 1)
            pool.wait_ge(consts, 3)

            def normed(n, i):
                rows = ITEM[i][1]
                pool.wait_ge(raw_copied, KQ * n + (i + 1))
                pool.wait_ge(rinv_made, n * 2 + (i // 2 + 1))
                wait(pool, p_hi_made, KQ * n + (i - 1))
                wait(pool, p_lo_made, KQ * n + (i - 1))
                nc.gpsimd.tensor_tensor(kn[i % 2][0:rows, :].rearrange("p (h d) -> p h d", d=HD),
                                        k_raw[i][0:rows, :].rearrange("p (h d) -> p h d", d=HD),
                                        rinv[0:rows, i, :].unsqueeze(2).broadcast_to([rows, H, HD]), ALU.mult).then_inc(kn_made, 1)

            def layer_scale(t, mv, out, var_made, stat_made, scale_made):
                pool.wait_ge(stat_made, (t + 1) * 2)
                nc.gpsimd.tensor_tensor(out[:, 0:1], mv[:, 1:2], ln_eps[0:N, :], ALU.add).then_inc(var_made, 1)
                pool.wait_ge(var_made, t + 1)
                nc.gpsimd.tensor_tensor(out[:, 1:2], out[:, 0:1], minus_half[0:N, 0:1], ALU.pow).then_inc(scale_made, 1)

            def one(b, par, n, c, m):
                if c is not None:
                    layer_scale(c, mv_h, rstd_hb, var_h, bn_h, rstd_h)
                    pool.wait_ge(x1_made, c + 1)
                    nc.gpsimd.dma_start(xres[:, :], x[bass.ds(c + 1, 1)].rearrange("o t d -> (o t) d")).then_inc(xres_in, 16)
                if n is not None:
                    normed(n, 2)
                    normed(n, 3)
                if m is not None:
                    layer_scale(m, mv_x, rstd_xb, var_x, bn_x, rstd_x)
                    normed(m, 0)
                    normed(m, 1)

            layer_scale(0, mv_x, rstd_xb, var_x, bn_x, rstd_x)
            pool.wait_ge(w_hi_made, 4)
            nc.gpsimd.tensor_tensor(w_parts[1][:, 2, :, :], w_raw[:, 2, :, :], w_parts[0][:, 2, :, :].bitcast(F32),
                                    ALU.subtract).then_inc(w_lo_made[2], 1)
            normed(0, 0)
            normed(0, 1)
            batches(pool, one)
            layer_scale(B - 1, mv_h, rstd_hb, var_h, bn_h, rstd_h)

        @block.scalar
        def _(act):
            act.wait_ge(consts, 2)
            nc.scalar.activation(guess[:, 0, 0:1], guess_bias[:, :], ACT.Exp).then_inc(table_loaded, 1)
            act.wait_ge(table_loaded, 1)

            def split_w(j):
                act.wait_ge(w_in[j], 16)
                if j > 0:
                    nc.scalar.activation(w_parts[0][:, j, :, :], w_raw[:, j, :, :], ACT.Copy).then_inc(w_hi_made, 1)
                else:
                    for k in (0, 2):
                        nc.scalar.activation(w_parts[0][:, j, k:k + 2, :], w_raw[:, j, k:k + 2, :], ACT.Copy).then_inc(w_hi_made, 1)

            def exps(b, j):
                rows = MT[j % 3][1]
                act.wait_ge(scores_done, b * UNITS + (j + 1))
                wait(act, pv_done, b * UNITS + (j - 1))
                nc.scalar.activation(probs[j % 2][0:rows, :].rearrange("p (a t) -> p a t", a=2),
                                     s_bank[0:rows, :, 0:4 * N], ACT.Exp, scale=float(HD) ** -0.5 * UNIT ** -2)\
                  .then_inc(probs_made, 1)

            def squares(n, i):
                rows = ITEM[i][1]
                act.wait_ge(kq_done, KQ * n + (i + 1))
                wait(act, ss_made, KQ * n + (i - 1))
                nc.scalar.activation(sq[i % 2][0:rows, :], kq_bank[0:rows, i % 2, :], ACT.Square,
                                     scale=float(HD) ** -0.5).then_inc(sq_made, 1)
                wait(act, kn_made, KQ * (n - 1) + (i + 1))
                nc.scalar.activation(k_raw[i][0:rows, :], kq_bank[0:rows, i % 2, :], ACT.Copy).then_inc(raw_copied, 1)

            def rsqrt_guess(n, r):
                act.wait_ge(ms_made, n * 2 + (r + 1))
                nc.scalar.activation(guess[:, :, :], ms[:, :, :].bitcast(mybir.dt.int32), ACT.Exp, scale=GUESS_SCALE,
                                     bias=guess_bias[:, :]).then_inc(guess_made, 1)

            def part_hi(n, i):
                step, rows = ITEM[i]
                act.wait_ge(kn_made, KQ * n + (i + 1))
                wait(act, tr_done, parts_free(n, i))
                src = kn[i % 2][0:rows, :].rearrange("p (h d) -> p h d", d=HD).unsqueeze(2).broadcast_to([rows, H, 2, HD])
                dst = stack4[i % 2][0:rows, :, 0:4:2, :] if step else stack4[i % 2][0:rows, :, 0:2, :]
                nc.scalar.activation(dst, src, ACT.Copy).then_inc(p_hi_made, 1)

            def copy_v(n, mt, par):
                rows = MT[mt][1]
                act.wait_ge(v_done, n * 3 + (mt + 1))
                wait(act, pv_done, (n - 1) * UNITS)
                if isinstance(n, int):
                    act.wait_ge(consts, 8)
                nc.scalar.activation(v_ext[par][0:rows, mt, :, 0:HD], v_bank[0:rows, :].rearrange("p (h d) -> p h d", d=HD),
                                     ACT.Copy).then_inc(v_copied, 1)

            def q_block(n, r, par):
                act.wait_ge(tr_done, n * TR + (8 + r))
                wait(act, scores_done, (n - 1) * UNITS)
                src = tr_bank[:, :].rearrange("p (a t) -> p a t", a=8)
                for h in range(2):
                    last = nc.scalar.activation(q_blk[par][64 * h:64 * h + 64, 8 * r:8 * r + 8, h * N:(h + 1) * N],
                                                src[64 * h:64 * h + 64, :, 0:N], ACT.Copy)
                last.then_inc(tr_used, 1)

            def x_high(n):
                act.wait_ge(xt_made, n + 1)
                wait(act, kq_done, n * KQ)
                nc.scalar.activation(x_parts[0][:, :, :], xt[:, :, :], ACT.Copy).then_inc(x_hi_made, 1)

            def context_hi(m, r):
                act.wait_ge(ctx_in, (m + 1) * 16)
                wait(act, v_done, (m - 1) * 3 + (2 + r))
                wait(act, kq_done, (m - 1) * KQ + (2 + r))
                cols = slice(CT, M) if r else slice(0, CT)
                nc.scalar.activation(c_parts[0][:, :, cols], c_raw[:, :, cols], ACT.Copy).then_inc(c_hi_made, 1)

            def one(b, par, n, c, m):
                q = 1 - par
                for j in range(UNITS):
                    if b is not None:
                        exps(b, j)
                    if n is not None:
                        first = is_first(n)
                        if j == 0:
                            part_hi(n, 0)
                            if not first:
                                x_high(n)
                            squares(n, 2)
                        if j == 1:
                            if first:
                                squares(n, 3)
                                rsqrt_guess(n, 1)
                            part_hi(n, 1)
                            copy_v(n, 0, q)
                        if j == 2 and not first:
                            squares(n, 3)
                        if j == 3 and not first:
                            rsqrt_guess(n, 1)
                        if j == 4:
                            part_hi(n, 2)
                            copy_v(n, 1, q)
                        if j == 5:
                            part_hi(n, 3)
                            if first:
                                copy_v(n, 2, q)
                        if j == 6 and not first:
                            copy_v(n, 2, q)
                        if j == 8:
                            q_block(n, 0, q)
                        if j == 9:
                            q_block(n, 1, q)
                    if m is not None:
                        if j == 5:
                            context_hi(m, 0)
                        if j == 7:
                            context_hi(m, 1)
                        if j == 8:
                            squares(m, 0)
                        if j == 10:
                            squares(m, 1)
                        if j == 11:
                            rsqrt_guess(m, 0)
                    if c is not None:
                        tail(c, j)

            def tail(c, j):
                if j == 4:
                    act.wait_ge(ht_made, c + 1)
                    nc.scalar.activation(h_parts[0][:, :, bass.ds(c * N, N)], ht[:, :, :], ACT.Copy).then_inc(h_hi_made, 1)
                if j == 8:
                    act.wait_ge(negm_made, c + 1)
                    nc.scalar.activation(pexp[:, :], lg[:, :], ACT.Exp, bias=neg_m[:, :],
                                         accum_out=pinv[:, 0:1]).then_inc(pexp_made, 1)

            split_w(0)
            split_w(1)
            act.wait_ge(c_lo_made, 1)
            context_hi(0, 1)
            split_w(2)
            squares(0, 0)
            squares(0, 1)
            rsqrt_guess(0, 0)
            x_high(0)
            batches(act, one)

            def split_gu(i, p):
                act.wait_ge(gu_in[p % WR], loads(i, p) * 16)
                nc.scalar.activation(gu_parts[p % WR][0][:, :, :, :].rearrange("p a k f -> p (a k f)"),
                                     raw_gu[p % WR][:, :], ACT.Copy).then_inc(gu_hi_made, 1)

            split_gu(0, 0)
            split_gu(0, 1)
            for j in range(UNITS):
                tail(B - 1, j)
            act.wait_ge(cw_made, B)

            def silu(t, half):
                act.wait_ge(g_done, t * 2 + (half + 1))
                wait(act, gu_mult, t * 2 + (half - 1))
                nc.scalar.activation(act_g[half][:, :], g_bank[:, half, 0:NH], ACT.Silu).then_inc(silu_made, 1)

            def tile(i, p):
                t = i * PER + p
                if p + 2 < PER or not isinstance(i, int) or i < ITER - 1:
                    split_gu(i + (p + 2) // PER, (p + 2) % PER)
                for half in range(2):
                    silu(t, half)
                    act.wait_ge(af_made, t * 2 + (half + 1))
                    nc.scalar.activation(a_parts[HSLOT[p]][0][:, half * NH:(half + 1) * NH], act_f[half][:, :],
                                         ACT.Copy).then_inc(a_hi_made, 1)
                act.wait_ge(dn_in[p % WR], loads(i, p) * 16)
                nc.scalar.activation(dn_parts[HSLOT[p]][0][:, :], raw_dn[p % WR][:, :], ACT.Copy).then_inc(dn_hi_made, 1)

            hidden_tiles(act, tile, lambda i, g: None)

        @block.vector
        def _(dve):
            def split_w(j, k0, k1):
                dve.wait_ge(w_hi_made, 1 + k0 // 2 if j == 0 else j + 2)
                nc.vector.tensor_tensor(w_parts[1][:, j, k0:k1, :], w_raw[:, j, k0:k1, :], w_parts[0][:, j, k0:k1, :].bitcast(F32),
                                        ALU.subtract).then_inc(w_lo_made[j], 1)

            def sums(n, i):
                rows = ITEM[i][1]
                dve.wait_ge(sq_made, KQ * n + (i + 1))
                if isinstance(n, int):
                    dve.wait_ge(consts, 4)
                nc.vector.tensor_reduce(ss[0:rows, i, :], sq[i % 2][0:rows, :].rearrange("p (h d) -> p h d", d=HD),
                                        AX.X, ALU.add).then_inc(ss_made, 1)

            def variances(n, r):
                dve.wait_ge(ss_made, KQ * n + 2 * (r + 1))
                nc.vector.tensor_scalar(ms[:, :, :], ss[:, 2 * r:2 * r + 2, :], RMS_EPS, UNIT ** -2, ALU.add, ALU.mult).then_inc(ms_made, 1)

            def rsqrt(n, r):
                dve.wait_ge(guess_made, n * 2 + (r + 1))
                wait(dve, kn_made, KQ * (n - 1) + 2 * (r + 1))
                t = (n * 2 + r) * 5
                y = guess
                for k, out in enumerate((nt[2], rinv)):
                    nc.vector.scalar_tensor_tensor(nt[0][:, :, :], ms[:, :, :], -0.5, y[:, :, :], ALU.mult, ALU.mult).then_inc(newton, 1)
                    dve.wait_ge(newton, t + (3 * k + 1))
                    nc.vector.tensor_tensor(nt[1][:, :, :], nt[0][:, :, :], y[:, :, :], ALU.mult).then_inc(newton, 1)
                    dve.wait_ge(newton, t + (3 * k + 2))
                    last = nc.vector.scalar_tensor_tensor(out[:, :, :] if k == 0 else rinv[:, 2 * r:2 * r + 2, :],
                                                          nt[1][:, :, :], 1.5, y[:, :, :], ALU.add, ALU.mult)
                    if k == 0:
                        last.then_inc(newton, 1)
                        dve.wait_ge(newton, t + 3)
                    y = out
                last.then_inc(rinv_made, 1)

            def part_lo(n, i):
                q, rows = ITEM[i]
                dve.wait_ge(p_hi_made, KQ * n + (i + 1))
                src = kn[i % 2][0:rows, :].rearrange("p (h d) -> p h d", d=HD).unsqueeze(2).broadcast_to([rows, H, 2, HD])
                hi = stack4[i % 2][0:rows, :, 0:4:2, :] if q else stack4[i % 2][0:rows, :, 0:2, :]
                lo = stack4[i % 2][0:rows, :, 1:4:2, :] if q else stack4[i % 2][0:rows, :, 2:4, :]
                nc.vector.tensor_tensor(lo, src, hi, ALU.subtract).then_inc(p_lo_made, 1)

            def k_block(n, mt, r, par, which):
                r0, rows = MT[mt]
                dve.wait_ge(tr_done, n * TR + which)
                wait(dve, scores_done, (n - 1) * UNITS)
                nc.vector.tensor_copy(k_t[par][:, 8 * r:8 * r + 8, r0:r0 + rows],
                                      tr_bank[:, :].rearrange("p (a t) -> p a t", a=8)[:, :, 0:rows]).then_inc(tr_used, 1)

            def o_norm(b, g, par):
                dve.wait_ge(pv_done, b * UNITS + 3 * (g + 1))
                acc = o_bank[0:N, g % 2, 0:GH * HV].rearrange("p (h v) -> p h v", v=HV)
                wait(dve, o_normed, b * HG + (g - 1))
                nc.vector.reciprocal(o_inv[:, g % 2, :].unsqueeze(2), acc[:, :, HD:HV]).then_inc(o_inv_made, 1)
                dve.wait_ge(o_inv_made, b * HG + (g + 1))
                nc.vector.tensor_tensor(x1[par][:, g * GH * HD:(g + 1) * GH * HD].rearrange("p (h d) -> p h d", d=HD),
                                        acc[:, :, 0:HD], o_inv[:, g % 2, :].unsqueeze(2).broadcast_to([N, GH, HD]),
                                        ALU.mult).then_inc(o_normed, 1)

            def layer_stats(t, src, stats, mv, made):
                nc.vector.bn_stats(stats[:, :], src).then_inc(made, 1)
                dve.wait_ge(made, t * 2 + 1)
                carry_wait()
                nc.vector.bn_aggr(mv[:, :], stats[:, :]).then_inc(made, 1)

            def one(b, par, n, c, m):
                q = 1 - par
                for j in range(UNITS):
                    if n is not None and j == 0:
                        if not is_first(n):
                            xt_copy(n)
                        part_lo(n, 0)
                    if b is not None and j in (4, 7, 10):
                        o_norm(b, j // 3 - 1, par)
                    if c is not None and j in (0, 5):
                        tail(c, j, q)
                    if n is not None:
                        prepare(n, j, q)
                    if c is not None and j not in (0, 5):
                        tail(c, j, q)
                    if n is not None and j == 3 and not is_first(n):
                        rsqrt(n, 1)
                    if m is not None:
                        if j == (6 if is_first(n) else 5):
                            context_lo(m, 0)
                        if j == 7:
                            context_lo(m, 1)
                        if j == 8:
                            x_stats(m)
                            sums(m, 0)
                        if j == 10:
                            sums(m, 1)
                            x_normed(m)
                        if j == 11:
                            variances(m, 0)
                            rsqrt(m, 0)

            def xt_copy(n):
                dve.wait_ge(tr_done, n * TR + 1)
                wait(dve, x_hi_made, n)
                nc.vector.tensor_copy(xt[:, :, :].rearrange("p k t -> p (k t)"),
                                      tr_bank[:, :].bitcast(F32)[:, 0:KT * N]).then_inc(xt_made, 1)

            def x_low(n):
                dve.wait_ge(x_hi_made, n + 1)
                nc.vector.tensor_tensor(x_parts[1][:, :, :], xt[:, :, :], x_parts[0][:, :, :].bitcast(F32),
                                        ALU.subtract).then_inc(x_lo_made, 1)

            def prepare(n, j, q):
                first = is_first(n)
                if j == 0 and not first:
                    x_low(n)
                if j == 1:
                    if first:
                        sums(n, 2)
                        sums(n, 3)
                        variances(n, 1)
                        k_block(n, 0, 0, q, 2)
                        part_lo(n, 1)
                    else:
                        k_block(n, 0, 0, q, 2)
                        part_lo(n, 1)
                        sums(n, 2)
                if j == 2:
                    k_block(n, 0, 1, q, 3)
                    if first:
                        rsqrt(n, 1)
                    else:
                        sums(n, 3)
                        variances(n, 1)
                if j == 3:
                    k_block(n, 1, 0, q, 4)
                if j == 4:
                    k_block(n, 1, 1, q, 5)
                    part_lo(n, 2)
                if j == 5:
                    part_lo(n, 3)
                if j == 6:
                    k_block(n, 2, 0, q, 6)
                if j == 7:
                    k_block(n, 2, 1, q, 7)

            def context_lo(m, r):
                dve.wait_ge(c_hi_made, m * 2 + (1 + r))
                cols = slice(CT, M) if r else slice(0, CT)
                nc.vector.tensor_tensor(c_parts[1][:, :, cols], c_raw[:, :, cols], c_parts[0][:, :, cols].bitcast(F32),
                                        ALU.subtract).then_inc(c_lo_made, 1)

            def x_stats(m):
                dve.wait_ge(x_in, (m + 1) * 16)
                layer_stats(m, xin[:, :], stats_x, mv_x, bn_x)

            def x_normed(m):
                dve.wait_ge(rstd_x, m + 1)
                nc.vector.tensor_scalar(xn[:, :], xin[:, :], mv_x[:, 0:1], rstd_xb[:, 1:2],
                                        ALU.subtract, ALU.mult).then_inc(xn_made, 1)

            def tail(c, j, par):
                if j == 0:
                    o_norm(c, 3, par)
                    dve.wait_ge(xres_in, (c + 1) * 16)
                    dve.wait_ge(o_normed, (c + 1) * HG)
                    nc.vector.tensor_tensor(x1[par][:, :], x1[par][:, :], xres[:, :], ALU.add).then_inc(x1_made, 1)
                    dve.wait_ge(x1_made, c + 1)
                    layer_stats(c, x1[par][:, :], stats_h, mv_h, bn_h)
                if j == 1:
                    dve.wait_ge(rstd_h, c + 1)
                    nc.vector.tensor_scalar(hn[:, :], x1[par][:, :], mv_h[:, 0:1], rstd_hb[:, 1:2],
                                            ALU.subtract, ALU.mult).then_inc(hn_made, 1)
                if j == 3:
                    dve.wait_ge(ht_done, c + 1)
                    nc.vector.tensor_copy(ht[:, :, :].rearrange("p k t -> p (k t)"), v_bank[:, 0:KT * N]).then_inc(ht_made, 1)
                if j == 4:
                    dve.wait_ge(h_hi_made, c + 1)
                    nc.vector.tensor_tensor(h_parts[1][:, :, bass.ds(c * N, N)], ht[:, :, :],
                                            h_parts[0][:, :, bass.ds(c * N, N)].bitcast(F32), ALU.subtract).then_inc(h_lo_made, 1)
                if j == 5:
                    dve.wait_ge(x1t_done, c + 1)
                    nc.vector.tensor_copy(y_sum[:, :, bass.ds(c * N, N)],
                                          v_bank[:, 0:KT * N].rearrange("p (k t) -> p k t", k=KT)).then_inc(x1t_made, 1)
                if j == 7:
                    dve.wait_ge(lg_done, c + 1)
                    nc.vector.tensor_copy(lg[:, :], v_bank[0:N, 0:E]).then_inc(lg_made, 1)
                    dve.wait_ge(lg_made, c + 1)
                    carry_wait()
                    nc.vector.max(top_l[:, :], lg[:, :]).then_inc(gate_step, 1)
                    dve.wait_ge(gate_step, c * 5 + 1)
                    nc.vector.tensor_scalar(neg_m[:, :], top_l[:, 0:1], -1.0, None, ALU.mult).then_inc(negm_made, 1)
                if j == 8:
                    dve.wait_ge(pexp_made, c + 1)
                    nc.vector.reciprocal(pinv[:, 1:2], pinv[:, 0:1]).then_inc(gate_step, 1)
                    dve.wait_ge(gate_step, c * 5 + 2)
                    nc.vector.tensor_scalar(sc_ext[:, 0:E], pexp[:, :], pinv[:, 1:2], None, ALU.mult).then_inc(gate_step, 1)
                    dve.wait_ge(gate_step, c * 5 + 3)
                    dve.wait_ge(consts, 12)
                    carry_wait()
                    nc.vector.max(top_l[:, :], sc_ext[:, 0:E]).then_inc(gate_step, 1)
                    dve.wait_ge(gate_step, c * 5 + 4)
                    nc.vector.tensor_copy(top_s[:, 0:TOP_K], top_l[:, 0:TOP_K]).then_inc(gate_step, 1)
                    dve.wait_ge(gate_step, c * 5 + 5)
                    carry_wait()
                    nc.vector.match_replace(rest[:, :], top_s[:, :], sc_ext[:, :], 0.0).then_inc(rest_made, 1)
                    dve.wait_ge(rest_made, c + 1)
                    nc.vector.tensor_tensor(cw[:, :], sc_ext[:, 0:E], rest[:, 0:E], ALU.subtract).then_inc(cw_made, 1)
                if j == 11:
                    dve.wait_ge(cwt_done, c + 1)
                    nc.vector.tensor_copy(cw_t[:, bass.ds(c * N, N)], v_bank[0:E, 0:N]).then_inc(cwt_made, 1)

            nc.vector.memset(carrier[:, :], 0.0).then_inc(cwt_made, 1)
            split_w(0, 0, 2)
            dve.wait_ge(ctx_in, 16)
            nc.vector.tensor_copy(c_parts[0][:, :, 0:CT], c_raw[:, :, 0:CT]).then_inc(c_hi_made, 1)
            context_lo(0, 0)
            split_w(0, 2, KT)
            x_stats(0)
            x_normed(0)
            context_lo(0, 1)
            split_w(1, 0, KT)
            sums(0, 0)
            sums(0, 1)
            variances(0, 0)
            xt_copy(0)
            rsqrt(0, 0)
            x_low(0)
            dve.wait_ge(eye_in, 16)
            nc.vector.tensor_copy(id16[:, :], id32[:, :]).then_inc(id16_made, 1)
            batches(dve, one)

            def split_gu(i, p):
                dve.wait_ge(gu_hi_made, i * PER + (p + 1))
                nc.vector.tensor_tensor(gu_parts[p % WR][1][:, :, :, :].rearrange("p a k f -> p (a k f)"), raw_gu[p % WR][:, :],
                                        gu_parts[p % WR][0][:, :, :, :].rearrange("p a k f -> p (a k f)").bitcast(F32),
                                        ALU.subtract).then_inc(gu_lo_made, 1)

            split_gu(0, 0)
            split_gu(0, 1)
            for j in range(UNITS):
                tail(B - 1, j, 1)

            def tile(i, p):
                t = i * PER + p
                if p + 2 < PER or not isinstance(i, int) or i < ITER - 1:
                    split_gu(i + (p + 2) // PER, (p + 2) % PER)
                for half in range(2):
                    k = t * 2 + (half + 1)
                    cols = slice(half * NH, (half + 1) * NH)
                    dve.wait_ge(silu_made, k)
                    dve.wait_ge(u_done, k)
                    nc.vector.tensor_tensor(act_u[half][:, :], act_g[half][:, :], u_bank[:, half, 0:NH], ALU.mult).then_inc(gu_mult, 1)
                    dve.wait_ge(gu_mult, k)
                    wait(dve, a_hi_made, k - 2)
                    segments = cw_segments(p)
                    for n, (r0, r1, e) in enumerate(segments):
                        dve.wait_ge(cwb_in[e], (i + 1) * 16)
                        last = nc.vector.tensor_tensor(act_f[half][r0:r1, :], act_u[half][r0:r1, :], cw_b[e][r0:r1, cols], ALU.mult)
                    last.then_inc(af_made, 1)
                    dve.wait_ge(a_hi_made, k)
                    a = a_parts[HSLOT[p]]
                    nc.vector.tensor_tensor(a[1][:, cols], act_f[half][:, :], a[0][:, cols].bitcast(F32),
                                            ALU.subtract).then_inc(a_lo_made, 1)
                dve.wait_ge(dn_hi_made, t + 1)
                d = dn_parts[HSLOT[p]]
                nc.vector.tensor_tensor(d[1][:, :], raw_dn[p % WR][:, :], d[0][:, :].bitcast(F32),
                                        ALU.subtract).then_inc(dn_lo_made, 1)

            def add_group(i, g):
                for idx in range(2 * KT):
                    dt, half = idx // 2, idx % 2
                    k = i * (6 * KT) + (2 * KT * g + idx + 1)
                    dve.wait_ge(y_done, k)
                    y = y_sum[:, dt, half * NH:(half + 1) * NH]
                    nc.vector.tensor_tensor(y, y, y_bank[:, idx % 4, 0:NH], ALU.add).then_inc(y_added, 1)

            hidden_tiles(dve, tile, add_group)

        @block.tensor
        def _(pe):
            def project(out, rows, lhs, w, col, halves=False, ks=range(KT)):
                for k in ks:
                    if halves and k % 2 == 0:
                        pe.wait_ge(w_lo_made[w], k // 2 + 1)
                    for s, (a, b) in enumerate(CASES):
                        last = nc.tensor.matmul(out, lhs[a][:, k, col:col + rows], w_parts[b][:, w, k, :],
                                                start=(k == 0 and s == 0), stop=(k == KT - 1 and s == 2))
                return last

            def project_k(n, mt, i, ks=range(KT)):
                if mt == 0 or mt == 2:
                    pe.wait_ge(c_hi_made, n * 2 + (1 if mt == 0 else 2))
                    pe.wait_ge(c_lo_made, n * 2 + (1 if mt == 0 else 2))
                wait(pe, raw_copied, KQ * n + (i - 1))
                last = project(kq_bank[0:MT[mt][1], i % 2, :], MT[mt][1], c_parts, 0, MT[mt][0],
                               halves=is_first(n) and mt == 0, ks=ks)
                if ks[-1] == KT - 1:
                    last.then_inc(kq_done, 1)

            def project_q(n):
                pe.wait_ge(x_hi_made, n + 1)
                pe.wait_ge(x_lo_made, n + 1)
                pe.wait_ge(w_lo_made[2], 1)
                wait(pe, raw_copied, KQ * n + 2)
                project(kq_bank[0:N, 1, :], N, x_parts, 2, 0).then_inc(kq_done, 1)

            def project_v(n, mt):
                pe.wait_ge(w_lo_made[1], 1)
                project(v_bank[0:MT[mt][1], :], MT[mt][1], c_parts, 1, MT[mt][0]).then_inc(v_done, 1)

            def bank_free(n, which):
                if which == 1:
                    pe.wait_ge(xt_made, n + 1)
                else:
                    wait(pe, tr_used, n * (TR - 1) + max(which - 1, 0))

            def x_transposes(n):
                pe.wait_ge(xn_made, n + 1)
                pe.wait_ge(eye_in, 16)
                bank_free(n, 0)
                for k in range(KT):
                    last = nc.tensor.transpose(tr_bank[:, :].bitcast(F32)[:, k * N:(k + 1) * N],
                                               xn[:, k * P:(k + 1) * P], id32[0:N, 0:N])
                last.then_inc(tr_done, 1)

            def stack_transposes(n, i, r, which):
                rows = ITEM[i][1]
                pe.wait_ge(id16_made, 1)
                pe.wait_ge(p_lo_made, KQ * n + (i + 1))
                bank_free(n, which)
                for a in range(8):
                    pair = stack4[i % 2][0:rows, 2 * (8 * r + a):2 * (8 * r + a) + 2, :, :].rearrange("p h s d -> p (h s d)")
                    last = nc.tensor.transpose(tr_bank[:, a * P:a * P + rows], pair, id16[0:rows, 0:rows])
                last.then_inc(tr_done, 1)

            def scores(b, j, par):
                g, mt = j // 3, j % 3
                r0, rows = MT[mt]
                wait(pe, probs_made, b * UNITS + j)
                if j == 0:
                    pe.wait_ge(tr_used, (b + 1) * (TR - 1))
                    pe.wait_ge(xt_made, b + 1)
                for a in range(4):
                    last = nc.tensor.matmul(s_bank[0:rows, a // 2, (a % 2) * 2 * N:(a % 2 + 1) * 2 * N],
                                            k_t[par][:, 4 * g + a, r0:r0 + rows], q_blk[par][:, 4 * g + a, :],
                                            start=True, stop=True)
                last.then_inc(scores_done, 1)

            def values(b, j, par):
                g, mt = j // 3, j % 3
                rows = MT[mt][1]
                pe.wait_ge(probs_made, b * UNITS + (j + 1))
                if j == 0:
                    pe.wait_ge(v_copied, (b + 1) * 3)
                if mt == 0:
                    wait(pe, o_normed, b * HG + (g - 1))
                for h in range(GH):
                    last = nc.tensor.matmul(o_bank[0:N, g % 2, h * HV:(h + 1) * HV], probs[j % 2][0:rows, h * N:(h + 1) * N],
                                            v_ext[par][0:rows, mt, g * GH + h, :], start=(mt == 0 and h == 0), stop=(mt == 2),
                                            skip_group_check=True)
                last.then_inc(pv_done, 1)

            def one(b, par, n, c, m):
                q = 1 - par
                for j in range(UNITS):
                    if b is not None:
                        scores(b, j, par)
                    if n is not None and j == 0:
                        if not is_first(n):
                            x_transposes(n)
                        project_k(n, 2, 2, range(2, KT))
                    if c is not None and j == 0:
                        values(c, UNITS - 1, q)
                    if n is not None:
                        first = is_first(n)
                        if j == 1:
                            if first:
                                project_q(n)
                            wait(pe, v_copied, n * 3)
                            if c is not None:
                                pe.wait_ge(cwt_made, c + 1)
                            project_v(n, 0)
                        if j == 2:
                            if not first:
                                project_q(n)
                            stack_transposes(n, 0, 1, 2)
                            if first:
                                pe.wait_ge(v_copied, 1)
                                project_v(n, 1)
                        if j == 3:
                            stack_transposes(n, 1, 0, 3)
                            pe.wait_ge(v_copied, n * 3 + 1)
                        if j == 4:
                            if c is not None:
                                pe.wait_ge(ht_made, c + 1)
                            if not first:
                                project_v(n, 1)
                            stack_transposes(n, 1, 1, 4)
                            if first:
                                pe.wait_ge(v_copied, 2)
                                project_v(n, 2)
                        if j == 5:
                            pe.wait_ge(v_copied, n * 3 + 2)
                        if j == 6:
                            stack_transposes(n, 2, 0, 5)
                            if c is not None:
                                pe.wait_ge(x1t_made, c + 1)
                            if not first:
                                project_v(n, 2)
                        if j == 7:
                            stack_transposes(n, 2, 1, 6)
                            pe.wait_ge(v_copied, n * 3 + 3)
                        if j == 8:
                            stack_transposes(n, 3, 0, 7)
                        if j == 9:
                            stack_transposes(n, 3, 1, 8)
                    if m is not None:
                        if j in (7, 8):
                            project_k(m, 0, 0, range(2 * (j - 7), 2 * (j - 7) + 2))
                        if j in (9, 10):
                            project_k(m, 1, 1, range(2 * (j - 9), 2 * (j - 9) + 2))
                        if j == 11:
                            project_k(m, 2, 2, range(0, 2))
                    if c is not None:
                        tail(c, j, q)
                    if b is not None and j > 0:
                        values(b, j - 1, par)
                    if n is not None and j == 1:
                        stack_transposes(n, 0, 0, 1)

            def tail(c, j, par):
                if j == 3:
                    pe.wait_ge(hn_made, c + 1)
                    for k in range(KT):
                        last = nc.tensor.transpose(v_bank[:, k * N:(k + 1) * N], hn[:, k * P:(k + 1) * P], id32[0:N, 0:N])
                    last.then_inc(ht_done, 1)
                if j == 5:
                    pe.wait_ge(ht_made, c + 1)
                    for k in range(KT):
                        last = nc.tensor.transpose(v_bank[:, k * N:(k + 1) * N], x1[par][:, k * P:(k + 1) * P], id32[0:N, 0:N])
                    last.then_inc(x1t_done, 1)
                if j == 7:
                    pe.wait_ge(x1t_made, c + 1)
                    pe.wait_ge(gate_in, 16)
                    for k in range(KT):
                        last = nc.tensor.matmul(v_bank[0:N, 0:E], ht[:, k, :], gate_w[:, k, :], start=(k == 0), stop=(k == KT - 1))
                    last.then_inc(lg_done, 1)
                if j == 11:
                    pe.wait_ge(lg_made, c + 1)
                    pe.wait_ge(cw_made, c + 1)
                    nc.tensor.transpose(v_bank[0:E, 0:N], cw[:, :], id32[0:N, 0:N]).then_inc(cwt_done, 1)

            project_k(0, 0, 0)
            project_k(0, 1, 1)
            x_transposes(0)
            project_k(0, 2, 2, range(0, 2))
            batches(pe, one)
            values(B - 1, UNITS - 1, 1)

            def gate_or_up(i, p, half, up):
                t = i * PER + p
                pe.wait_ge(gu_lo_made, t + 1)
                w = gu_parts[p % WR]
                bank, freed, done = (u_bank, gu_mult, u_done) if up else (g_bank, silu_made, g_done)
                wait(pe, freed, t * 2 + (half - 1))
                for k in range(KT):
                    for m, (a, b) in enumerate(CASES):
                        last = nc.tensor.matmul(bank[:, half, 0:NH], w[a][:, up, k, :], h_parts[b][:, k, half * NH:(half + 1) * NH],
                                                start=(k == 0 and m == 0), stop=(k == KT - 1 and m == 2))
                last.then_inc(done, 1)

            pe.wait_ge(probs_made, B * UNITS)
            gate_or_up(0, 0, 0, 0)
            tail(B - 1, 3, 1)
            gate_or_up(0, 0, 0, 1)
            tail(B - 1, 5, 1)
            tail(B - 1, 7, 1)
            pe.wait_ge(h_hi_made, B)
            pe.wait_ge(h_lo_made, B)
            gate_or_up(0, 0, 1, 0)
            tail(B - 1, 11, 1)
            gate_or_up(0, 0, 1, 1)

            def tile(i, p):
                if not (isinstance(i, int) and i == 0 and p == 0):
                    for half in range(2):
                        gate_or_up(i, p, half, 0)
                        gate_or_up(i, p, half, 1)

            def contract(g, idx, first, end):
                dt, half = idx // 2, idx % 2
                begin, close = GROUPS[g]
                for p in range(first, end):
                    for m, (a, b) in enumerate(CASES):
                        last = nc.tensor.matmul(y_bank[:, idx % 4, 0:NH], dn_parts[HSLOT[p]][a][:, dt * P:(dt + 1) * P],
                                                a_parts[HSLOT[p]][b][:, half * NH:(half + 1) * NH],
                                                start=(p == begin and m == 0), stop=(p == close - 1 and m == 2))
                return last

            def down(i, g):
                first, end = GROUPS[g]
                t_end = i * PER + end
                if isinstance(i, int) and i == ITER - 1 and g == len(GROUPS) - 1:
                    pe.wait_ge(a_lo_made, (t_end - 1) * 2)
                    pe.wait_ge(dn_lo_made, t_end - 1)
                    for idx in range(4):
                        contract(g, idx, first, end - 1)
                    ahead = 4
                else:
                    ahead = 0
                pe.wait_ge(a_lo_made, t_end * 2)
                pe.wait_ge(dn_lo_made, t_end)
                for idx in range(2 * KT):
                    if idx >= 4:
                        pe.wait_ge(y_added, i * (6 * KT) + (2 * KT * g + idx - 3))
                    contract(g, idx, end - 1 if idx < ahead else first, end).then_inc(y_done, 1)

            hidden_tiles(pe, tile, down)


def kernel(x, ctx_2048, L0_xattn_Wq, L0_xattn_Wk, L0_xattn_Wv, L0_ffn_gate_w, L0_ffn_w_gate, L0_ffn_w_up, L0_ffn_w_down):
    import concourse.bacc as bacc
    import numpy as np
    from concourse.bass_utils import run_bass_kernel_spmd

    B, N, D = x.shape
    M = ctx_2048.shape[1]
    E, F, _ = L0_ffn_w_gate.shape
    KT, TILES = D // P, E * F // P

    def k_major(w):
        return np.asarray(w).T.reshape(KT, P, -1).transpose(1, 0, 2)

    kv = np.concatenate([np.asarray(L0_xattn_Wk), np.asarray(L0_xattn_Wv)], axis=0)
    w_kvq = np.stack([k_major(kv[0::2]), k_major(kv[1::2]), k_major(L0_xattn_Wq)], axis=1)
    ctx_t = np.asarray(ctx_2048).transpose(0, 2, 1).reshape(B, KT, P, M).transpose(0, 2, 1, 3)

    def hidden_major(w):
        return np.asarray(w).reshape(TILES, P, KT, P).transpose(0, 3, 2, 1).reshape(TILES, P, KT * P)

    down = np.asarray(L0_ffn_w_down).transpose(0, 2, 1).reshape(TILES, P, D)
    w_moe = np.concatenate([hidden_major(L0_ffn_w_gate), hidden_major(L0_ffn_w_up), down], axis=2)

    ins = {
        "x": np.asarray(x), "ctx_t": ctx_t, "w_kvq": w_kvq, "gate_t": k_major(L0_ffn_gate_w), "w_moe": w_moe,
        "eye": np.eye(P, dtype=np.float32),
    }
    ins = {f"in_{name}": np.ascontiguousarray(a) for name, a in ins.items()}
    nc = bacc.Bacc("TRN2", target_bir_lowering=False, num_devices=1)
    aps = [nc.dram_tensor(name, a.shape, mybir.dt.from_np(a.dtype), kind="ExternalInput").ap() for name, a in ins.items()]
    out = nc.dram_tensor("out_t", (KT, P, B * N), F32, kind="ExternalOutput").ap()
    xattn_moe_program(nc, *aps, out)
    r = run_bass_kernel_spmd(nc, [ins], core_ids=[0])
    return r.results[0]["out_t"].reshape(D, B * N).T.reshape(B, N, D)
```
